# Optimizing a Trainium2 kernel written in Bass

```python
import numpy as np
import jax
import jax.numpy as jnp

def _softmax(x, axis=-1):
    return jax.nn.softmax(x, axis=axis)

def _gelu(x):
    return jax.nn.gelu(x, approximate=True)

def _silu(x):
    return jax.nn.silu(x)

def _sigmoid(x):
    return jax.nn.sigmoid(x)

def _layernorm(x, axis=-1, eps=1e-05):
    m = jnp.mean(x, axis=axis, keepdims=True)
    v = jnp.var(x, axis=axis, keepdims=True)
    return (x - m) / jnp.sqrt(v + eps)

def _scatter_add(tgt, idx, src, axis=0):
    return tgt.at[idx].add(src)

def _segment_sum(src, seg, n):
    return jax.ops.segment_sum(src, seg, n)
kernel_name = 'mk_flamingo_gated_d1_seqx_r4_252ca5'

def setup_inputs(seed: int=0):
    np.random.seed(seed)
    _w = jnp.asarray

    def _rec_inputs():
        import jax
        import jax.numpy as jnp
        _rk = jax.random.key(seed)
        x = -0.0003929 + 0.9999 * jax.random.normal(jax.random.fold_in(_rk, 1), (16, 100, 512), jnp.float32)
        _lenS = 100 - jax.random.randint(jax.random.fold_in(_rk, 7), (16,), 0, max(1, 100 // 4) + 1, jnp.int32)
        _lenS2 = 361 - jax.random.randint(jax.random.fold_in(_rk, 8), (16,), 0, max(1, 361 // 4) + 1, jnp.int32)
        _ctx_2048P = jax.random.normal(jax.random.fold_in(_rk, 11), (16, 16, 512), jnp.float32)
        _ctx_2048c = jax.random.dirichlet(jax.random.fold_in(_rk, 511), 0.3 * jnp.ones((16,), jnp.float32), (16, 361))
        _ctx_2048t = jnp.einsum('bsk,bkd->bsd', _ctx_2048c, _ctx_2048P)
        _ctx_2048t = _ctx_2048t * jax.lax.rsqrt(jnp.mean(jnp.square(_ctx_2048t)) + 1e-12) * 0.953939
        ctx_2048 = -0.000514642 + 1.00011 * (_ctx_2048t + 0.3 * jax.random.normal(jax.random.fold_in(_rk, 611), (16, 361, 512), jnp.float32))
        _g = jax.random.normal(jax.random.fold_in(_rk, 9001), (2, 1), jnp.float32)
        _g = jnp.sign(_g) * jnp.maximum(jnp.abs(_g), 1.0) + (_g == 0) * 1.0
        g_xattn = _g[0]
        g_ffn = _g[1]
        return (x, ctx_2048, g_xattn, g_ffn)
    x, ctx_2048, g_xattn, g_ffn = _rec_inputs()

    def _L0_xattn_setup():
        import jax, jax.numpy as jnp
        import numpy as np
        DIM = 512
        NHEADS = 32
        HEAD_DIM = DIM // NHEADS
        EPS = 1e-06

        def _rmsnorm(t):
            return t * jax.lax.rsqrt(jnp.mean(t * t, axis=-1, keepdims=True) + EPS)
        key = jax.random.key(seed)
        kx, kc, kq, kk, kv = jax.random.split(key, 5)
        x = jax.random.normal(kx, (2, 1024, DIM), dtype=jnp.float32)
        context = jax.random.normal(kc, (2, 128, DIM), dtype=jnp.float32)
        std = 0.02
        Wq = jax.random.normal(kq, (DIM, DIM), dtype=jnp.float32) * std
        Wk = jax.random.normal(kk, (DIM, DIM), dtype=jnp.float32) * std
        Wv = jax.random.normal(kv, (DIM, DIM), dtype=jnp.float32) * std
        return {'x': x, 'context': context, 'Wq': Wq, 'Wk': Wk, 'Wv': Wv}
    _L0_xattn_all = _L0_xattn_setup()
    _L0_xattn_in = {k: v for k, v in _L0_xattn_all.items() if k in ('Wq', 'Wk', 'Wv')}
    del _L0_xattn_all

    def _L0_ffn_setup():
        import jax, jax.numpy as jnp
        import numpy as np
        B, S, D, F, E, K = (2, 512, 512, 1024, 8, 1)

        def _silu_mul(gu):
            g, u = jnp.split(gu, 2, axis=-1)
            return jax.nn.silu(g) * u

        def _moe_forward(hidden_states, router_w, w_gate_up, w_down, shared_gate_up, shared_down, top_k=K):
            b, s, d = hidden_states.shape
            x = hidden_states.reshape(-1, d)
            router_logits = x @ router_w.T
            topk_vals, topk_ids = jax.lax.top_k(router_logits, top_k)
            gate = jax.nn.sigmoid(topk_vals.astype(jnp.float32)).astype(x.dtype)
            xs = (x[:, None, :] * gate[:, :, None]).reshape(-1, d)
            ids_flat = topk_ids.reshape(-1)
            n_experts = w_gate_up.shape[0]

            def body(acc, inp):
                wg, wd, e = inp
                h = _silu_mul(xs @ wg)
                o = h @ wd
                mask = (ids_flat == e)[:, None]
                return (acc + jnp.where(mask, o, jnp.zeros((), o.dtype)), None)
            acc0 = jnp.zeros_like(xs)
            routed, _ = jax.lax.scan(body, acc0, (w_gate_up, w_down, jnp.arange(n_experts)))
            routed = routed.reshape(-1, top_k, d).sum(1)
            shared = _silu_mul(x @ shared_gate_up) @ shared_down
            return (routed + shared).reshape(b, s, d)
        key = jax.random.key(seed)
        ks = jax.random.split(key, 6)
        scale = 0.02
        return {'hidden_states': jax.random.normal(ks[0], (B, S, D), jnp.float32), 'router_w': jax.random.normal(ks[1], (E, D), jnp.float32) * scale, 'w_gate_up': jax.random.normal(ks[2], (E, D, 2 * F), jnp.float32) * scale, 'w_down': jax.random.normal(ks[3], (E, F, D), jnp.float32) * scale, 'shared_gate_up': jax.random.normal(ks[4], (D, 2 * F), jnp.float32) * scale, 'shared_down': jax.random.normal(ks[5], (F, D), jnp.float32) * scale}
    _L0_ffn_all = _L0_ffn_setup()
    _L0_ffn_in = {k: v for k, v in _L0_ffn_all.items() if k in ('router_w', 'w_gate_up', 'w_down', 'shared_gate_up', 'shared_down')}
    del _L0_ffn_all
    return {'x': x, 'ctx_2048': ctx_2048, 'g_xattn': g_xattn, 'g_ffn': g_ffn, 'L0_xattn_Wq': _L0_xattn_in['Wq'], 'L0_xattn_Wk': _L0_xattn_in['Wk'], 'L0_xattn_Wv': _L0_xattn_in['Wv'], 'L0_ffn_router_w': _L0_ffn_in['router_w'], 'L0_ffn_w_gate_up': _L0_ffn_in['w_gate_up'], 'L0_ffn_w_down': _L0_ffn_in['w_down'], 'L0_ffn_shared_gate_up': _L0_ffn_in['shared_gate_up'], 'L0_ffn_shared_down': _L0_ffn_in['shared_down']}

def reference(x, ctx_2048, g_xattn, g_ffn, L0_xattn_Wq, L0_xattn_Wk, L0_xattn_Wv, L0_ffn_router_w, L0_ffn_w_gate_up, L0_ffn_w_down, L0_ffn_shared_gate_up, L0_ffn_shared_down):
    import jax
    import jax.numpy as jnp

    def _L0_xattn_ref(x, context, Wq, Wk, Wv):
        import jax, jax.numpy as jnp
        import numpy as np
        DIM = 512
        NHEADS = 32
        HEAD_DIM = DIM // NHEADS
        EPS = 1e-06

        def _rmsnorm(t):
            return t * jax.lax.rsqrt(jnp.mean(t * t, axis=-1, keepdims=True) + EPS)
        b, n, _ = x.shape
        m = context.shape[1]
        q = x @ Wq.T
        k_raw = context @ Wk.T
        v_raw = context @ Wv.T
        q = q.reshape(b, n, NHEADS, HEAD_DIM).transpose(0, 2, 1, 3)
        kv = jnp.concatenate([k_raw, v_raw], axis=-1)
        kv = kv.reshape(b, m, NHEADS, HEAD_DIM, 2)
        k = kv[..., 0].transpose(0, 2, 1, 3)
        v = kv[..., 1].transpose(0, 2, 1, 3)
        q = _rmsnorm(q)
        k = _rmsnorm(k)
        scale = HEAD_DIM ** (-0.5)
        scores = jnp.einsum('bhnd,bhmd->bhnm', q, k) * scale
        attn = jax.nn.softmax(scores, axis=-1)
        out = jnp.einsum('bhnm,bhmd->bhnd', attn, v)
        return out.transpose(0, 2, 1, 3).reshape(b, n, NHEADS * HEAD_DIM)

    def _L0_ffn_ref(hidden_states, router_w, w_gate_up, w_down, shared_gate_up, shared_down):
        import jax, jax.numpy as jnp
        import numpy as np
        B, S, D, F, E, K = (2, 512, 512, 1024, 8, 1)

        def _silu_mul(gu):
            g, u = jnp.split(gu, 2, axis=-1)
            return jax.nn.silu(g) * u

        def _moe_forward(hidden_states, router_w, w_gate_up, w_down, shared_gate_up, shared_down, top_k=K):
            b, s, d = hidden_states.shape
            x = hidden_states.reshape(-1, d)
            router_logits = x @ router_w.T
            topk_vals, topk_ids = jax.lax.top_k(router_logits, top_k)
            gate = jax.nn.sigmoid(topk_vals.astype(jnp.float32)).astype(x.dtype)
            xs = (x[:, None, :] * gate[:, :, None]).reshape(-1, d)
            ids_flat = topk_ids.reshape(-1)
            n_experts = w_gate_up.shape[0]

            def body(acc, inp):
                wg, wd, e = inp
                h = _silu_mul(xs @ wg)
                o = h @ wd
                mask = (ids_flat == e)[:, None]
                return (acc + jnp.where(mask, o, jnp.zeros((), o.dtype)), None)
            acc0 = jnp.zeros_like(xs)
            routed, _ = jax.lax.scan(body, acc0, (w_gate_up, w_down, jnp.arange(n_experts)))
            routed = routed.reshape(-1, top_k, d).sum(1)
            shared = _silu_mul(x @ shared_gate_up) @ shared_down
            return (routed + shared).reshape(b, s, d)
        return _moe_forward(hidden_states, router_w, w_gate_up, w_down, shared_gate_up, shared_down)
    x = x + jnp.tanh(g_xattn[0]) * _L0_xattn_ref(_layernorm(x, axis=-1), ctx_2048, L0_xattn_Wq, L0_xattn_Wk, L0_xattn_Wv)
    x = x + jnp.tanh(g_ffn[0]) * _L0_ffn_ref(_layernorm(x, axis=-1), L0_ffn_router_w, L0_ffn_w_gate_up, L0_ffn_w_down, L0_ffn_shared_gate_up, L0_ffn_shared_down)
    return x

_drawn_inputs = setup_inputs


def setup_inputs(seed=0):
    import zlib

    import numpy as np

    out = dict(_drawn_inputs(seed))
    spreads = {}
    factors = {}
    for name, (base, spread) in spreads.items():
        noise = np.random.default_rng([zlib.crc32(name.encode()), seed]).standard_normal(out[name].shape)
        drawn = base * np.exp(spread * noise) if base else spread * noise
        out[name] = jnp.asarray(drawn.astype(out[name].dtype))
    for name, factor in factors.items():
        out[name] = (out[name] * factor).astype(out[name].dtype)
    return out
```

```python
from contextlib import ExitStack

import concourse.bass as bass
from concourse import mybir

F32 = mybir.dt.float32
F32R = mybir.dt.float32r
F16 = mybir.dt.float16
I32 = mybir.dt.int32
U32 = mybir.dt.uint32
ALU = mybir.AluOpType
ACT = mybir.ActivationFunctionType
AX = mybir.AxisListType

P = 128
LN_EPS = 1e-5
RMS_EPS = 1e-6
RSQRT_MAGIC = 0x5F3759DF


class Counter:

    def __init__(self, sem):
        self.sem, self.value = sem, 0

    def mark(self, instruction, by=1):
        instruction.then_inc(self.sem, by)
        self.value += by
        return self, self.value


class Waits:

    def __init__(self):
        self.seen = {}

    def __call__(self, engine, *marks):
        for mark in marks:
            if mark is None:
                continue
            counter, value = mark
            key = (engine.engine, counter.sem.name)
            if self.seen.get(key, 0) < value:
                engine.wait_ge(counter.sem, value)
                self.seen[key] = value


def rsqrt_step(nc, wait, done, y, t, x, ready, i):
    v = nc.vector
    wait(v, ready)
    if i == 0:
        return done.mark(v.tensor_scalar(y.bitcast(I32), x.bitcast(I32), -0.5, float(RSQRT_MAGIC),
                                         ALU.mult, ALU.add))
    if i % 3 == 1:
        return done.mark(v.tensor_tensor(t, y, y, ALU.mult))
    if i % 3 == 2:
        return done.mark(v.scalar_tensor_tensor(out=t, in0=t, scalar=-0.5, in1=x,
                                                op0=ALU.mult, op1=ALU.mult))
    return done.mark(v.scalar_tensor_tensor(out=y, in0=t, scalar=1.5, in1=y,
                                            op0=ALU.add, op1=ALU.mult))


RSQRT_STEPS = 10

T_SLOTS = (-3, 2, 8, 16)
RMS_SLOTS = (1, 2, 2, 2, 3, 3, 4, 4, 5, 5, 5)
PACK_SLOTS = (6, 8, 10, 14)
PACK_T_SLOTS = (10, 12, 14, 18)


def rsqrt_steps(nc, wait, done, y, t, x, ready):
    for i in range(RSQRT_STEPS):
        ready = rsqrt_step(nc, wait, done, y, t, x, ready, i)
    return ready


def build_program(nc, x, ctx, g_xattn, g_ffn, w_q, w_k, w_v, w_router, w_gate_up, w_down,
                  w_sh_gate_up, w_sh_down, out, stage="all"):
    B, N, D = x.shape
    M = ctx.shape[1]
    HD = 16
    H = D // HD
    KD = D // P
    HPAIR = H // 2
    HROW = P // 2
    GH = 4
    NG = H // GH
    MT = [(r, min(P, M - r)) for r in range(0, M, P)]
    NMT = len(MT)
    VW = 2 * HD + 1
    SCALE = float(HD) ** -0.5
    MULT, ADD, SUB = ALU.mult, ALU.add, ALU.subtract

    stack = ExitStack()
    with stack:
        def sb(name, shape, dt, scope=None):
            return (scope or stack).enter_context(nc.sbuf_tensor(name, shape, dt))

        def counter(name):
            return Counter(stack.enter_context(nc.semaphore(name)))

        bank = [stack.enter_context(nc.psum_tensor(f"bank{i}", [P, 512], F32)) for i in range(8)]
        wait = Waits()
        pe, act, dve, pool = (counter(n) for n in ("pe_done", "act_done", "dve_done", "pool_done"))
        PE, ACTE, DVE, POOL, SP = nc.tensor, nc.scalar, nc.vector, nc.gpsimd, nc.sync

        ident32 = sb("ident32", [P, P], F32)
        ident16 = sb("ident16", [P, P], F16)
        gates = sb("gates", [P, 2], F32)
        x_all = sb("x_all", [N, B, D], F32)
        ln_stats = sb("ln_stats", [N, B, 6], F32)
        ln_mv = sb("ln_mv", [N, B, 2], F32)
        ln_var = sb("ln_var", [N, B], F32)
        ln_rstd = sb("ln_rstd", [N, B], F32)
        ln_tmp = sb("ln_tmp", [N, B], F32)

        m = pool.mark(POOL.memset(ident32[:], 0.0))
        wait(POOL, m)
        identity_ready = pool.mark(POOL.affine_select(
            out=ident32[:], in_=ident32[:], compare_op=ALU.not_equal, fill=1.0, base=0,
            pattern=[[-1, P]], channel_multiplier=1))
        wait(DVE, identity_ready)
        identity16_ready = dve.mark(DVE.tensor_copy(ident16[:], ident32[:]))

        x_in = [counter(f"x_in{i}") for i in range(4)]
        XC = B // len(x_in)
        x_ready = [x_in[i].mark(ACTE.dma_start(
            x_all[:, XC * i:XC * i + XC, :], x[XC * i:XC * i + XC].rearrange("b n d -> n b d")), 16)
            for i in range(len(x_in))]
        g_in = counter("g_in")
        for i, g in enumerate((g_xattn, g_ffn)):
            g_ready = g_in.mark(ACTE.dma_start(
                gates[:, i:i + 1], g.rearrange("(a n) -> a n", a=1).to_broadcast([P, 1])), 16)
        wait(ACTE, g_ready)
        gates_ready = act.mark(ACTE.activation(gates[:], gates[:], ACT.Tanh))

        def layer_norm_stats(b0, nb, ready):
            wait(DVE, ready)
            for b in range(b0, b0 + nb):
                m = dve.mark(DVE.bn_stats(ln_stats[:, b, :], x_all[:, b, :]))
            wait(DVE, m)
            for b in range(b0, b0 + nb):
                m = dve.mark(DVE.bn_aggr(ln_mv[:, b, :], ln_stats[:, b, :]))
            wait(DVE, m)
            s = slice(b0, b0 + nb)
            m = dve.mark(DVE.tensor_scalar(ln_var[:, s], ln_mv[:, s, 1], LN_EPS, None, ADD))
            return rsqrt_steps(nc, wait, dve, ln_rstd[:, s], ln_tmp[:, s], ln_var[:, s], m)

        x1_done = [None] * B
        attention(locals())
        if stage == "x1":
            st = counter("stores")
            wait(SP, *x1_done)
            s = st.mark(SP.dma_start(out.rearrange("b n d -> n b d"), x_all[:]), 16)
            wait(SP, s)
            return
        nc.all_engine_barrier()
        feed_forward(locals())


def attention(env):
    (nc, stack, sb, counter, bank, wait, pe, act, dve, pool, PE, ACTE, DVE, POOL, SP, B, N, D, M, HD,
     H, KD, HPAIR, HROW, GH, NG, MT, NMT, VW, SCALE, MULT, ADD, SUB) = (env[k] for k in (
        "nc stack sb counter bank wait pe act dve pool PE ACTE DVE POOL SP B N D M HD H KD HPAIR "
        "HROW GH NG MT NMT VW SCALE MULT ADD SUB").split())
    ident32, ident16, identity_ready, identity16_ready = (
        env[k] for k in "ident32 ident16 identity_ready identity16_ready".split())
    x_all, ln_mv, ln_rstd, gates, gates_ready, x_ready, XC, x1_done, ctx = (
        env[k] for k in "x_all ln_mv ln_rstd gates gates_ready x_ready XC x1_done ctx".split())
    scope = ExitStack()
    with scope:
        def buf(name, shape, dt):
            return sb(name, shape, dt, scope)

        wqT = [buf(f"wqT_{p}", [P, KD, D], F32R) for p in ("hi", "lo")]
        wkvT = [buf(f"wkvT_{p}", [P, KD, 2, D], F32R) for p in ("hi", "lo")]
        NRAW = 6
        raw = [buf(f"raw{i}", [P, D], F32) for i in range(NRAW)]
        raw_in = [counter(f"raw_in{i}") for i in range(NRAW)]
        raw_free = [None] * NRAW
        srcT = [[buf(f"srcT_{p}{i}", [P, KD, P], F32R) for p in ("hi", "lo")] for i in range(2)]
        srcT_free = [None] * 2
        xn = buf("xn", [N, D], F32)
        square = buf("square", [P, D], F32)
        k_raw = buf("k_raw", [P, NMT, D], F32)
        q_raw = buf("q_raw", [N, D], F32)
        sumsq = [buf(f"sumsq{i}", [P, NMT + 1, H], F32) for i in range(2)]
        rms = [buf(f"rms{i}", [P, NMT + 1, H], F32) for i in range(2)]
        rms_tmp = buf("rms_tmp", [P, NMT + 1, H], F32)
        normed = [buf(f"normed{i}", [P, D], F32) for i in range(2)]
        k_pack = [buf(f"k_pack{t}", [P, H, HROW], F16) for t in range(NMT)]
        q_pack = buf("q_pack", [N, H, HROW], F16)
        kT = [buf(f"kT{i}", [P, HPAIR, NMT * P], F16) for i in range(2)]
        qT = [buf(f"qT{i}", [P, HPAIR, 2 * N], F16) for i in range(2)]
        v_pack = [buf(f"v_pack{i}", [P, NMT, H, VW], F16) for i in range(3)]
        NPR = 3
        probs = [buf(f"probs{i}", [P, GH, N], F32) for i in range(NPR)]
        probs_hi = [buf(f"probs_hi{i}", [P, GH, P], F16) for i in range(NPR)]
        probs_lo = [buf(f"probs_lo{i}", [P, GH, P], F16) for i in range(NPR)]
        heads_out = buf("heads_out", [N, H, VW], F32)
        inv_sum = buf("inv_sum", [N, H], F32)

        for t in k_pack + [q_pack] + qT + probs_hi + probs_lo:
            m = pool.mark(POOL.memset(t[:], 0.0))
        for t in v_pack:
            m = pool.mark(POOL.memset(t[:, :, :, HD:HD + 1], 1.0))
        for t in sumsq:
            m = pool.mark(POOL.memset(t[:], 1.0))
        constants_ready = m

        bank_free = [None] * 8

        n_raw = 0

        def load_rows(src):
            nonlocal n_raw
            i = n_raw % NRAW
            n_raw += 1
            wait(SP, raw_free[i])
            ready = raw_in[i].mark(SP.dma_start(raw[i][0:src.shape[0], :], src), 16)
            return i, ready

        weights = [(w, j) for w in ("w_q", "w_k", "w_v") for j in range(KD)]
        pending = [load_rows(env[w][P * j:P * j + P, :]) for w, j in weights[:NRAW]]
        wait(PE, identity_ready)
        for n, (w, j) in enumerate(weights):
            i, ready = pending[n]
            bk = (0, 2, 3, 4, 5, 6)[n % 6]
            wait(PE, ready, bank_free[bk])
            for k in range(KD):
                tr = PE.transpose(bank[bk][:, P * k:P * k + P], raw[i][:, P * k:P * k + P], ident32[:])
            transposed = pe.mark(tr)
            raw_free[i] = transposed
            if w == "w_q":
                src = bank[bk][:].rearrange("p (k c) -> p k c", k=KD)
                dst = [t[:, :, P * j:P * j + P] for t in wqT]
            else:
                src = bank[bk][:].rearrange("p (k c s) -> p k s c", k=KD, s=2)
                c0 = (D // 2 if w == "w_v" else 0) + P // 2 * j
                dst = [t[:, :, :, c0:c0 + P // 2] for t in wkvT]
            wait(ACTE, transposed)
            hi = act.mark(ACTE.activation(dst[0], src, ACT.Copy))
            wait(DVE, hi)
            weights_ready = dve.mark(DVE.tensor_tensor(dst[1], src, dst[0].bitcast(F32), SUB))
            bank_free[bk] = weights_ready
            if n + NRAW < len(weights):
                w2, j2 = weights[n + NRAW]
                pending.append(load_rows(env[w2][P * j2:P * j2 + P, :]))

        env["layer_norm_stats"](0, XC, x_ready[0])
        for i in range(1, len(x_ready)):
            stats_ready = env["layer_norm_stats"](XC * i, XC, x_ready[i])

        ctx_tiles = [(b, t) for b in range(B) for t in range(NMT)]
        ctx_loaded = {}

        def prefetch_ctx():
            if len(ctx_loaded) < len(ctx_tiles):
                b, t = ctx_tiles[len(ctx_loaded)]
                r, m = MT[t]
                ctx_loaded[b, t] = load_rows(ctx[b, r:r + m, :])

        units = [(g, t) for g in range(NG) for t in range(NMT)]
        SLOTS = len(units)
        agenda = {}

        def at(slot, engine, step, *args):
            agenda.setdefault((slot, engine), []).append((step, args))

        mark = {}
        prj_ring, tr_ring = [0], [0]

        def next_prj_bank():
            prj_ring[0] += 1
            return (2, 3)[prj_ring[0] % 2]

        def next_tr_bank():
            tr_ring[0] += 1
            return (0, 1)[tr_ring[0] % 2]

        def transpose_source(slot, b, t):
            side = t % 2
            rows = MT[t][1] if t < NMT else N

            def on_pe():
                if t < NMT:
                    i, ready = ctx_loaded[b, t]
                    src = raw[i][0:rows, :]
                else:
                    src, ready = xn[:], mark["xn", b]
                bk = mark["bank", b, t] = next_tr_bank()
                wait(PE, ready, bank_free[bk])
                for k in range(KD):
                    tr = PE.transpose(bank[bk][:, P * k:P * k + rows], src[:, P * k:P * k + P],
                                      ident32[0:rows, 0:rows])
                mark["T", b, t] = transposed = pe.mark(tr)
                if t < NMT:
                    raw_free[i] = transposed
                    prefetch_ctx()
                else:
                    mark["xn free"] = transposed

            def views():
                psum = bank[mark["bank", b, t]][:].rearrange("p (k r) -> p k r", k=KD)[:, :, 0:rows]
                return psum, *(s[:, :, 0:rows] for s in srcT[side])

            def on_act():
                psum, hi, lo = views()
                wait(ACTE, mark["T", b, t], mark.get(("src free", side)))
                mark["src high", b, t] = act.mark(ACTE.activation(hi, psum, ACT.Copy))

            def on_dve():
                psum, hi, lo = views()
                wait(DVE, mark["src high", b, t])
                mark["src", b, t] = bank_free[mark["bank", b, t]] = dve.mark(
                    DVE.tensor_tensor(lo, psum, hi.bitcast(F32), SUB))

            at(slot, "pe", on_pe)
            at(slot + 1, "act", on_act)
            at(slot + 2, "dve", on_dve)

        def project(slots, b, t, weight):
            side = t % 2
            rows = MT[t][1] if t < NMT else N
            name = "prj", b, t, weight
            w = {"q": wqT, "k": [a[:, :, 0, :] for a in wkvT], "v": [a[:, :, 1, :] for a in wkvT]}[weight]
            products = [(k, a, c) for k in range(KD) for a, c in ((0, 0), (0, 1), (1, 0))]

            def on_pe(n):
                k, a, c = products[n]
                if n == 0:
                    mark["bank", name] = bk = next_prj_bank()
                    wait(PE, mark["src", b, t], bank_free[bk])
                mm = PE.matmul(bank[mark["bank", name]][0:rows, :], srcT[side][a][:, k, 0:rows],
                               w[c][:, k], start=(n == 0), stop=(n == len(products) - 1))
                if n == len(products) - 1:
                    mark[name] = mark["src free", side] = pe.mark(mm)

            for n, slot in enumerate(slots):
                at(slot, "pe", on_pe, n)

        def take_heads(slot, b, t, weight):
            rows, dst = (MT[t][1], k_raw[0:MT[t][1], t, :]) if t < NMT else (N, q_raw[:])
            name = "prj", b, t, weight

            def copy():
                wait(ACTE, mark[name], mark.get(("scaled", b - 1, t)))
                mark["raw", b, t] = act.mark(ACTE.activation(
                    dst, bank[mark["bank", name]][0:rows, :], ACT.Copy))

            def take_square():
                wait(ACTE, mark.get("square free"))
                mark["square"] = bank_free[mark["bank", name]] = act.mark(ACTE.activation(
                    square[0:rows, :], bank[mark["bank", name]][0:rows, :], ACT.Square))

            def reduce():
                wait(DVE, mark["square"], mark.get(("rms", b - 2)))
                mark["sumsq", b, t] = mark["square free"] = dve.mark(DVE.tensor_reduce(
                    sumsq[b % 2][0:rows, t, :],
                    square[0:rows, :].rearrange("p (h d) -> p h d", d=HD), AX.X, ADD))

            at(slot, "act", copy)
            at(slot, "act", take_square)
            at(slot + 1, "dve", reduce)

        def take_values(slot, b, t):
            name = "prj", b, t, "v"
            m = MT[t][1]
            vp = v_pack[b % 3][0:m, t]

            def psum():
                return bank[mark["bank", name]][0:m, :].rearrange("p (h d) -> p h d", d=HD)

            def on_act():
                wait(ACTE, mark[name], mark.get(("values", b - 3)))
                mark["v high", b, t] = act.mark(ACTE.activation(vp[:, :, 0:HD], psum(), ACT.Copy))

            def on_dve():
                wait(DVE, mark["v high", b, t])
                mark["v", b] = bank_free[mark["bank", name]] = dve.mark(
                    DVE.tensor_tensor(vp[:, :, HD + 1:VW], psum(), vp[:, :, 0:HD], SUB))

            at(slot, "act", on_act)
            at(slot + 1, "dve", on_dve)

        def normalise_x(slot, b):
            def on_dve():
                wait(DVE, stats_ready, mark.get("xn free"))
                mark["xn", b] = dve.mark(DVE.tensor_scalar(
                    xn[:], x_all[:, b, :], ln_mv[:, b, 0:1], ln_rstd[:, b:b + 1], SUB, MULT))
            at(slot, "dve", on_dve)

        def rms_factors(slots, b):
            s = sumsq[b % 2][:]

            def mean():
                wait(DVE, *[mark["sumsq", b, t] for t in range(NMT + 1)],
                     mark.get(("scaled", b - 2, NMT)))
                mark["rms", b] = dve.mark(DVE.tensor_scalar(s, s, 1.0 / HD, RMS_EPS, MULT, ADD))

            def step(i):
                mark["rms", b] = rsqrt_step(nc, wait, dve, rms[b % 2][:], rms_tmp[:], s,
                                            mark["rms", b], i)

            at(slots[0], "dve", mean)
            for i, slot in enumerate(slots[1:]):
                at(slot, "dve", step, i)

        def make_pack(slot, b, t):
            if t < NMT:
                rows, src, pack, places, low_place = MT[t][1], k_raw[:, t, :], k_pack[t], (0, 2 * HD), HD
            else:
                rows, src, pack, places, low_place = N, q_raw[:], q_pack, (0, HD), 2 * HD
            n = normed[t % 2][0:rows, :]
            nh = n.rearrange("p (h d) -> p h d", d=HD)

            def scale():
                wait(DVE, mark["rms", b], mark["raw", b, t], mark.get(("normed free", t % 2)))
                mark["scaled", b, t] = dve.mark(DVE.tensor_tensor(
                    nh, src[0:rows].rearrange("p (h d) -> p h d", d=HD),
                    rms[b % 2][0:rows, t, :].unsqueeze(2).to_broadcast([rows, H, HD]), MULT))

            def high():
                a, c = places
                wide = pack[0:rows, :, a:c + HD].rearrange(
                    "p h (s d) -> p h s d", d=HD)[:, :, ::(c - a) // HD, :]
                wait(ACTE, mark["scaled", b, t], mark.get(("pack transposed", b - 1, t)))
                mark["pack high", b, t] = act.mark(ACTE.activation(
                    wide, nh.unsqueeze(2).to_broadcast([rows, H, 2, HD]), ACT.Copy))

            def low():
                wait(DVE, mark["pack high", b, t])
                mark["pack", b, t] = mark["normed free", t % 2] = dve.mark(DVE.tensor_tensor(
                    pack[0:rows, :, low_place:low_place + HD], nh,
                    pack[0:rows, :, places[0]:places[0] + HD], SUB))

            at(slot, "dve", scale)
            at(slot + 1, "act", high)
            at(slot + 2, "dve", low)

        def transpose_pack(slot, b, t, half):
            pack, rows = (k_pack[t], P) if t < NMT else (q_pack, N)
            name = "bank", "pack", b, t, half
            pairs = slice(HPAIR // 2 * half, HPAIR // 2 * (half + 1))

            def psum():
                return bank[mark[name]][:].bitcast(F16).rearrange("p (a r) -> p a r", a=HPAIR // 2)

            def on_pe():
                bk = mark[name] = next_tr_bank()
                wait(PE, mark["pack", b, t], bank_free[bk])
                for a in range(HPAIR // 2):
                    pair = HPAIR // 2 * half + a
                    tr = PE.transpose(psum()[:, a, 0:rows], pack[0:rows, 2 * pair:2 * pair + 2, :]
                                      .rearrange("p a c -> p (a c)"), ident16[0:rows, 0:rows])
                mark["pack transposed", b, t] = mark["pack T", b, t, half] = pe.mark(tr)

            def on_act():
                wait(ACTE, mark["pack T", b, t, half], mark.get(("scored", b - 2)))
                if t < NMT:
                    m = act.mark(ACTE.activation(
                        kT[b % 2][:, pairs, P * t:P * t + P].bitcast(F32), psum().bitcast(F32), ACT.Copy))
                else:
                    for z in range(2):
                        rows_z = slice(HROW * z, HROW * z + HROW)
                        m = act.mark(ACTE.activation(
                            qT[b % 2][rows_z, pairs, N * z:N * z + N].bitcast(F32),
                            psum()[rows_z, :, 0:N].bitcast(F32), ACT.Copy))
                mark["kT", b] = bank_free[mark[name]] = m

            at(slot, "pe", on_pe)
            at(slot + 1, "act", on_act)

        def unit(s):
            return (s // SLOTS, *units[s % SLOTS]) if 0 <= s < B * SLOTS else None

        sc_banks, pv_banks = (4, 5), (6, 7)

        def scores(s):
            b, g, t = unit(s)
            bk = sc_banks[s % 2]
            wait(PE, mark["kT", b], bank_free[bk])
            for a in range(GH // 2):
                pair = GH // 2 * g + a
                mm = PE.matmul(bank[bk][:, 2 * N * a:2 * N * (a + 1)],
                               kT[b % 2][:, pair, P * t:P * t + P], qT[b % 2][:, pair, :],
                               start=True, stop=True)
            mark["scored", b] = mark["scores", s % 2] = pe.mark(mm)

        def exp_scores(s):
            bk = sc_banks[s % 2]
            wait(ACTE, mark["scores", s % 2], mark.get(("probs free", s % NPR)))
            mark["probs", s % NPR] = bank_free[bk] = act.mark(ACTE.activation(
                probs[s % NPR][:], bank[bk][:, 0:GH * N].rearrange("p (h n) -> p h n", h=GH),
                ACT.Exp, scale=SCALE))

        def split_high(s):
            i = s % NPR
            wait(DVE, mark["probs", i], mark.get(("split free", i)))
            mark["high", i] = dve.mark(DVE.tensor_copy(probs_hi[i][:, :, 0:N], probs[i][:]))

        def split_low(s):
            i = s % NPR
            wait(DVE, mark["high", i])
            mark["split", i] = mark["probs free", i] = dve.mark(DVE.tensor_tensor(
                probs_lo[i][:, :, 0:N], probs[i][:], probs_hi[i][:, :, 0:N], SUB))

        def weighted_values(s):
            b, g, t = unit(s)
            bk = pv_banks[g % 2]
            m = MT[t][1]
            i = s % NPR
            wait(PE, mark["split", i], mark["v", b], bank_free[bk])
            for h in range(GH):
                v = v_pack[b % 3][0:m, t, GH * g + h, :]
                col = VW * h
                PE.matmul(bank[bk][:, col:col + VW], probs_hi[i][0:m, h, :], v,
                          start=(t == 0 and h == 0), stop=False, skip_group_check=True)
                mm = PE.matmul(bank[bk][:, col:col + HD + 1], probs_lo[i][0:m, h, :], v[:, 0:HD + 1],
                               start=False, stop=(t == NMT - 1 and h == GH - 1),
                               skip_group_check=True)
            mark["split free", i] = mark["values", b] = pe.mark(mm)

        def take_outputs(b, g, heads_free):
            bk = pv_banks[g % 2]
            wait(ACTE, mark["values", b], heads_free())
            mark["heads", b] = bank_free[bk] = act.mark(ACTE.activation(
                heads_out[:, GH * g:GH * g + GH, :],
                bank[bk][0:N, 0:GH * VW].rearrange("p (h c) -> p h c", h=GH), ACT.Copy))

        def finish_attention(slot, b):
            o = heads_out[:, :, 0:HD]
            xb = x_all[:, b, :].rearrange("p (h d) -> p h d", d=HD)

            def invert():
                wait(DVE, mark["heads", b], gates_ready)
                mark["inv"] = dve.mark(DVE.reciprocal(inv_sum[:], heads_out[:, :, HD]))

            def add_parts():
                mark["o"] = dve.mark(DVE.tensor_tensor(o, heads_out[:, :, 0:HD],
                                                       heads_out[:, :, HD + 1:VW], ADD))

            def divide():
                wait(DVE, mark["inv"], mark["o"])
                mark["o"] = dve.mark(DVE.tensor_tensor(
                    o, o, inv_sum[:].unsqueeze(2).to_broadcast([N, H, HD]), MULT))

            def add_to_x():
                wait(DVE, mark["o"])
                x1_done[b] = mark["x1", b] = dve.mark(DVE.scalar_tensor_tensor(
                    out=xb, in0=o, scalar=gates[0:N, 0:1], in1=xb, op0=MULT, op1=ADD))

            at(slot, "dve", invert)
            at(slot, "dve", add_parts)
            at(slot + 1, "dve", divide)
            at(slot + 1, "dve", add_to_x)

        PJ = 3 * KD
        projections = [(t, w) for t in range(NMT) for w in ("v", "k")] + [(NMT, "q")]
        pj_slots = [n * SLOTS // (PJ * len(projections)) for n in range(PJ * len(projections))]
        for b in range(-2, B):
            w0 = SLOTS * b
            c, d = b + 1, b + 2
            if d < B:
                for t, slot in zip(range(NMT + 1), T_SLOTS):
                    transpose_source(w0 + slot, d, t)
                normalise_x(w0 + T_SLOTS[NMT] - 2, d)
                for i, (t, weight) in enumerate(projections):
                    slots = pj_slots[PJ * i:PJ * i + PJ]
                    project([w0 + s for s in slots], d, t, weight)
                    if weight == "v":
                        take_values(w0 + slots[-1] + 1, d, t)
                    else:
                        take_heads(w0 + slots[-1] + 1, d, t, weight)
                rms_factors([w0 + SLOTS + s for s in RMS_SLOTS], d)
            if 0 <= c < B:
                for t in range(NMT + 1):
                    make_pack(w0 + PACK_SLOTS[t], c, t)
                    for half in range(2):
                        transpose_pack(w0 + PACK_T_SLOTS[t] + half, c, t, half)
            if b >= 0:
                for g in range(NG):
                    at(w0 + NMT * g + NMT - 1 + 3, "act", take_outputs, b, g,
                       lambda b=b: mark.get(("x1", b - 1)))
                finish_attention(w0 + SLOTS + 3, b)

        for _ in range(NRAW):
            prefetch_ctx()
        wait(PE, weights_ready, constants_ready, identity16_ready)
        wait(ACTE, constants_ready)
        wait(DVE, constants_ready)
        for s in range(min(slot for slot, _ in agenda), max(slot for slot, _ in agenda) + 1):
            if unit(s + 1):
                scores(s + 1)
            if unit(s):
                exp_scores(s)
            for step, args in agenda.get((s, "act"), []):
                step(*args)
            fills = agenda.get((s, "dve"), [])
            own = [(split_high, (s - 1,)), (split_low, (s - 1,))] if unit(s - 1) else []
            for i in range(max(len(fills), len(own))):
                for step, args in own[i:i + 1] + fills[i:i + 1]:
                    step(*args)
            for step, args in agenda.get((s, "pe"), []):
                step(*args)
            if unit(s - 2):
                weighted_values(s - 2)


def feed_forward(env):
    (nc, stack, sb, counter, bank, PE, ACTE, DVE, POOL, SP, B, N, D, KD, MULT, ADD, SUB) = (
        env[k] for k in "nc stack sb counter bank PE ACTE DVE POOL SP B N D KD MULT ADD SUB".split())
    wait, pe, act, dve, pool = (env[k] for k in "wait pe act dve pool".split())
    ident32, x_all, gates, out = (env[k] for k in "ident32 x_all gates out".split())
    ln_stats, ln_mv, ln_var, ln_rstd, ln_tmp = (
        env[k] for k in "ln_stats ln_mv ln_var ln_rstd ln_tmp".split())
    w_router, w_gate_up, w_down, w_sh_gate_up, w_sh_down = (
        env[k] for k in "w_router w_gate_up w_down w_sh_gate_up w_sh_down".split())
    E, F = w_down.shape[0], w_down.shape[1]
    T = B * N
    CT = 4
    NCH = B // CT
    CW = CT * N
    FQ = 256
    NQ = F // FQ
    KF = FQ // P
    SLOTS = 2 * P
    MAX_SWEEPS = -(-T // SLOTS)
    CAP = MAX_SWEEPS * SLOTS
    NT = SLOTS // P

    gated_rows = nc.dram_tensor("gated_rows", (T, D), F32).ap()
    routed_rows = nc.dram_tensor("routed_rows", (T, D), F32).ap()
    lists = nc.dram_tensor("expert_lists", (E * CAP, 1), I32).ap()

    scope = ExitStack()
    with scope:
        def buf(name, shape, dt):
            return sb(name, shape, dt, scope)

        xnT = [[buf(f"xnT_{p}{c}", [P, KD, CW], F32R) for p in ("hi", "lo")] for c in range(NCH)]
        NRAW = 4
        PART = P * D // P * 2
        raw = [buf(f"w_raw{i}", [P, PART], F32) for i in range(NRAW)]
        NUNIT = 3
        w_split = [[[buf(f"w{n}{s}_{p}", [P, PART], F32R) for p in ("hi", "lo")] for n in ("gate", "up", "down")]
                   for s in range(NUNIT)]
        hT = [[buf(f"hT_{p}{i}", [P, KF, CW], F32R) for p in ("hi", "lo")] for i in range(2)]
        hidden = [buf(f"hidden{i}", [P, CW], F32) for i in range(2)]
        rows = [buf(f"rows{i}", [P, D], F32) for i in range(4)]
        y_rows = [buf(f"y_rows{i}", [P, D], F32) for i in range(NT)]
        wrT = [buf(f"wrT_{p}", [P, KD, P], F32R) for p in ("hi", "lo")]
        logitsT = buf("logitsT", [E, CW], F32)
        logits = buf("logits", [N, CT, E], F32)
        top = buf("top", [N, CT, E], F32)
        top_index = buf("top_index", [N, CT, E], U32)
        expert = buf("expert", [N, CT], F32)
        gate = buf("gate", [N, CT], F32)
        gate_rstd = buf("gate_rstd", [N, CT], F32)
        onehot = buf("onehot", [N, CT, E], F16)
        counted = buf("counted", [N, 2, E], F16)
        chunk_count = buf("chunk_count", [N, E], F32)
        place = buf("place", [N, CT, E], F32)
        slot_f = buf("slot_f", [N, CT], F32)
        slot = buf("slot", [N, B], I32)
        token_id = buf("token_id", [N, B], I32)
        columns = buf("columns", [N, E], F32)
        list_base = buf("list_base", [N, E], F32)
        before = buf("before", [N, N], F16)
        ones16 = buf("ones16", [N, N], F16)
        sweep_edges = buf("sweep_edges", [1, MAX_SWEEPS], F32)
        sweeps_f = buf("sweeps_f", [1, 2], F32)
        sweeps = buf("sweeps", [1, 1], I32)
        none_fill = buf("none_fill", [P, E * CAP // P], I32)
        list_ids = buf("list_ids", [P, E, NT], I32)

        m = pool.mark(POOL.iota(token_id[:], [[N, B]], base=0, channel_multiplier=1))
        m = pool.mark(POOL.iota(columns[:], [[1, E]], base=0, channel_multiplier=0,
                                allow_small_or_imprecise_dtypes=True))
        m = pool.mark(POOL.iota(list_base[:], [[CAP, E]], base=0, channel_multiplier=0,
                                allow_small_or_imprecise_dtypes=True))
        m = pool.mark(POOL.iota(sweep_edges[:], [[SLOTS, MAX_SWEEPS]], base=0, channel_multiplier=0,
                                allow_small_or_imprecise_dtypes=True))
        m = pool.mark(POOL.iota(none_fill[:], [[0, E * CAP // P]], base=T, channel_multiplier=0))
        filled = m
        POOL.memset(ones16[:], 1.0)
        POOL.memset(counted[:], 0.0)
        for t in rows:
            m = pool.mark(POOL.memset(t[:], 0.0))
        wait(POOL, m)
        m = pool.mark(POOL.affine_select(out=before[:], in_=ones16[:], compare_op=ALU.is_gt, fill=0.0,
                                         base=0, pattern=[[1, N]], channel_multiplier=-1))
        constants_ready = m
        lists_io = counter("lists_io")
        wait(POOL, filled)
        lists_cleared = lists_io.mark(POOL.dma_start(
            lists.rearrange("(p c) o -> p (c o)", p=P), none_fill[:]), 16)

        def unit_parts(gate_up, down, q):
            g = gate_up.rearrange("(k p) f -> p k f", p=P)
            d = down.rearrange("(k p) n -> p k n", p=P)
            return [g[:, :, FQ * q:FQ * q + FQ], g[:, :, F + FQ * q:F + FQ * q + FQ],
                    d[:, KF * q:KF * q + KF, :]]

        class WeightStream:

            def __init__(self, parts, raw_in, wait, act, dve):
                self.parts, self.raw_in = parts, raw_in
                self.wait, self.act, self.dve = wait, act, dve
                self.loaded, self.n_split = [], 0
                self.raw_free = [None] * NRAW
                self.unit_free = [None] * NUNIT
                self.ready = {}
                self.load(NRAW)

            def load(self, n):
                for part in self.parts[len(self.loaded):len(self.loaded) + n]:
                    i = len(self.loaded) % NRAW
                    self.wait(SP, self.raw_free[i])
                    dst = raw[i][:].rearrange("p (a c) -> p a c", a=part.shape[1])
                    self.loaded.append(self.raw_in[i].mark(SP.dma_start(dst, part), 16))

            def split(self, n):
                for _ in range(min(n, len(self.parts) - self.n_split)):
                    part = self.n_split
                    self.n_split += 1
                    i = part % NRAW
                    u, which = divmod(part, 3)
                    hi, lo = w_split[u % NUNIT][which]
                    self.wait(ACTE, self.loaded[part], self.unit_free[u % NUNIT])
                    high = self.act.mark(ACTE.activation(hi[:], raw[i][:], ACT.Copy))
                    self.wait(DVE, high)
                    low = self.dve.mark(DVE.tensor_tensor(lo[:], raw[i][:], hi[:].bitcast(F32), SUB))
                    self.raw_free[i] = self.ready[part] = low
                    self.load(1)

        raw_in = [counter(f"w_raw_in{i}") for i in range(NRAW)]
        shared_w = WeightStream([p for q in range(NQ) for p in unit_parts(w_sh_gate_up, w_sh_down, q)],
                                raw_in, wait, act, dve)
        bank_free = [None] * 8
        n_bank = 0

        def next_bank():
            nonlocal n_bank
            n_bank += 1
            return (n_bank - 1) % 4

        def transpose_rows(src, n_rows, dst, ready, dst_free=None):
            bk = next_bank()
            wait(PE, ready, bank_free[bk])
            for k in range(KD):
                tr = PE.transpose(bank[bk][:, P * k:P * k + n_rows], src[:, P * k:P * k + P],
                                  ident32[0:n_rows, 0:n_rows])
            transposed = pe.mark(tr)
            psum = bank[bk][:].rearrange("p (k r) -> p k r", k=KD)[:, :, 0:n_rows]
            wait(ACTE, transposed, dst_free)
            high = act.mark(ACTE.activation(dst[0], psum, ACT.Copy))
            wait(DVE, high)
            low = dve.mark(DVE.tensor_tensor(dst[1], psum, dst[0].bitcast(F32), SUB))
            bank_free[bk] = low
            return low, transposed

        router_in = counter("router_in")
        wait(SP, constants_ready)
        router_loaded = router_in.mark(SP.dma_start(rows[0][0:E, :], w_router), 16)
        wait(DVE, constants_ready)
        for t in wrT:
            m = dve.mark(DVE.tensor_copy(t[:], rows[1][:].rearrange("p (k c) -> p k c", k=KD)))
        router_ready, transposed = transpose_rows(rows[0][0:E, :], E, [t[:, :, 0:E] for t in wrT],
                                                  router_loaded, m)
        rows_free = [transposed, None, None, None]
        n_rows = 0
        wait(PE, constants_ready)

        rows_out = [counter(f"rows_out{i}") for i in range(4)]
        table_io = counter("table_io")
        xnT_ready = [None] * NCH
        xs_done = [None] * NCH
        small_free = {}
        rank_seen = None

        def next_rows():
            nonlocal n_rows
            n_rows += 1
            i = (n_rows - 1) % 4
            wait(DVE, rows_free[i])
            return i

        def route(c):
            nonlocal rank_seen
            b0 = CT * c
            s = slice(b0, b0 + CT)
            rstd_ready = env["layer_norm_stats"](b0, CT, env["x1_done"][b0 + CT - 1])
            for j in range(CT):
                i = next_rows()
                wait(DVE, rstd_ready)
                normal = dve.mark(DVE.tensor_scalar(rows[i][0:N, :], x_all[:, b0 + j, :], ln_mv[:, b0 + j, 0:1],
                                                    ln_rstd[:, b0 + j:b0 + j + 1], SUB, MULT))
                xnT_ready[c], rows_free[i] = transpose_rows(
                    rows[i][0:N, :], N, [t[:, :, N * j:N * j + N] for t in xnT[c]], normal)
            bk = next_bank()
            wait(PE, xnT_ready[c], router_ready, bank_free[bk])
            for k in range(KD):
                for n, (a, x) in enumerate(((0, 0), (0, 1), (1, 0))):
                    mm = PE.matmul(bank[bk][:, 0:CW], wrT[a][:, k, :], xnT[c][x][:, k, :],
                                   start=(k == 0 and n == 0), stop=(k == KD - 1 and n == 2))
            m = pe.mark(mm)
            wait(ACTE, m, small_free.get("logitsT"))
            bank_free[bk] = m = act.mark(ACTE.activation(logitsT[:], bank[bk][0:E, 0:CW], ACT.Copy))
            bk = next_bank()
            wait(PE, m, bank_free[bk])
            for j in range(CT):
                tr = PE.transpose(bank[bk][0:N, E * j:E * j + E], logitsT[:, N * j:N * j + N],
                                  ident32[0:E, 0:E])
            m = small_free["logitsT"] = pe.mark(tr)
            wait(DVE, m, rank_seen)
            bank_free[bk] = m = dve.mark(DVE.tensor_copy(
                logits[:], bank[bk][0:N, 0:CT * E].rearrange("n (j e) -> n j e", j=CT)))
            wait(DVE, m)
            for j in range(CT):
                m = dve.mark(DVE.max(top[:, j, :], logits[:, j, :]))
            wait(DVE, m)
            top_ready = m
            for j in range(CT):
                m = dve.mark(DVE.max_index(top_index[:, j, :], top[:, j, :], logits[:, j, :]))
            wait(DVE, m)
            m = dve.mark(DVE.tensor_copy(expert[:], top_index[:, :, 0]))
            wait(DVE, m, rank_seen)
            hot = dve.mark(DVE.tensor_tensor(
                onehot[:], columns[:].unsqueeze(1).to_broadcast([N, CT, E]),
                expert[:].unsqueeze(2).to_broadcast([N, CT, E]), ALU.is_equal))
            wait(ACTE, top_ready)
            m = act.mark(ACTE.activation(gate[:], top[:, :, 0], ACT.Tanh, scale=0.5))
            wait(DVE, m)
            m = dve.mark(DVE.tensor_scalar(gate[:], gate[:], 0.5, 0.5, MULT, ADD))
            wait(DVE, m)
            m = dve.mark(DVE.tensor_tensor(gate_rstd[:], gate[:], ln_rstd[:, s], MULT))
            wait(DVE, m)
            for j in range(CT):
                i = next_rows()
                m = xs_done[c] = dve.mark(DVE.tensor_scalar(
                    rows[i][0:N, :], x_all[:, b0 + j, :], ln_mv[:, b0 + j, 0:1],
                    gate_rstd[:, j:j + 1], SUB, MULT))
                wait(POOL, m)
                t0 = N * (b0 + j)
                rows_free[i] = rows_out[i].mark(
                    POOL.dma_start(gated_rows[t0:t0 + N, :], rows[i][0:N, :]), 16)
            bk = next_bank()
            wait(PE, hot, bank_free[bk])
            done = counted[:, c % 2, :]
            for j in range(CT):
                o = bank[bk][0:N, E * j:E * j + E]
                terms = [(before, onehot[:, j, :])] + [(ones16, onehot[:, i, :]) for i in range(j)]
                terms.append((ones16, done))
                for n, (a, x) in enumerate(terms):
                    mm = PE.matmul(o, a[:], x, start=(n == 0), stop=(n == len(terms) - 1))
            ranked = pe.mark(mm)
            m = dve.mark(DVE.tensor_reduce(chunk_count[:], onehot[:].rearrange("n j e -> n e j"), AX.X, ADD))
            wait(DVE, m, ranked)
            counts_ready = dve.mark(DVE.tensor_tensor(counted[:, (c + 1) % 2, :], chunk_count[:], done, ADD))
            bank_free[bk] = m = dve.mark(DVE.tensor_tensor(
                place[:], bank[bk][0:N, 0:CT * E].rearrange("n (j e) -> n j e", j=CT),
                list_base[:].unsqueeze(1).to_broadcast([N, CT, E]), ADD))
            wait(DVE, m)
            m = dve.mark(DVE.tensor_tensor(place[:], place[:], onehot[:], MULT))
            rank_seen = m
            wait(DVE, m)
            m = dve.mark(DVE.tensor_reduce(slot_f[:], place[:], AX.X, ADD))
            wait(DVE, m)
            m = dve.mark(DVE.tensor_copy(slot[:, s], slot_f[:]))
            wait(POOL, m, lists_cleared)
            for b in range(b0, b0 + CT):
                m = table_io.mark(POOL.indirect_dma_start(
                    lists, bass.IndirectOffsetOnAxis(ap=slot[:, b:b + 1], axis=0),
                    token_id[:, b:b + 1], None), 16)
            wait(PE, counts_ready)
            return m, counts_ready

        def gate_up_product(n, wu, xs, width, w_ready, x_ready):
            hi, lo = (t[:, :, 0:width] for t in hT[n % 2])
            for j in range(KF):
                banks = []
                for which in range(2):
                    bk = next_bank()
                    banks.append(bk)
                    wait(PE, w_ready[which], x_ready, bank_free[bk])
                    w = [t[:].rearrange("p (k f) -> p k f", k=KD) for t in wu[which]]
                    for k in range(KD):
                        for i, (a, x) in enumerate(((0, 0), (0, 1), (1, 0))):
                            mm = PE.matmul(bank[bk][:, 0:width], w[a][:, k, P * j:P * j + P], xs[x][:, k, :],
                                           start=(k == 0 and i == 0), stop=(k == KD - 1 and i == 2))
                    m = pe.mark(mm)
                    h = hidden[j % 2][:, 0:width]
                    if which == 0:
                        wait(ACTE, m, hidden_free[j % 2])
                        m = bank_free[bk] = act.mark(ACTE.activation(h, bank[bk][:, 0:width], ACT.Silu))
                        wait(DVE, m)
                    else:
                        wait(DVE, m)
                        m = bank_free[bk] = dve.mark(DVE.tensor_tensor(h, bank[bk][:, 0:width], h, MULT))
                wait(ACTE, m, hT_free[n % 2])
                high = act.mark(ACTE.activation(hi[:, j, :], h, ACT.Copy))
                wait(DVE, high)
                hidden_free[j % 2] = low = dve.mark(DVE.tensor_tensor(
                    lo[:, j, :], h, hi[:, j, :].bitcast(F32), SUB))
            return low

        hidden_free = [None] * 2
        hT_free = [None] * 2

        def down_product(n, wd, r0, n_r, bk, w_ready, h_ready, first, last):
            hi, lo = hT[n % 2]
            wait(PE, w_ready, h_ready, bank_free[bk])
            w = [t[:].rearrange("p (k n) -> p k n", k=KF) for t in wd]
            for j in range(KF):
                for i, (h, a) in enumerate(((hi, 0), (hi, 1), (lo, 0))):
                    mm = PE.matmul(bank[bk][0:n_r, :], h[:, j, r0:r0 + n_r], w[a][:, j, :],
                                   start=(first and j == 0 and i == 0),
                                   stop=(last and j == KF - 1 and i == 2))
            return pe.mark(mm)

        shared_w.split(6)
        x2_done = [None] * B

        def shared_down(n, q, c, h_ready):
            for j in range(CT):
                b = CT * c + j
                bk = 4 + (CT * n + j) % 4
                m = down_product(n, w_split[q % NUNIT][2], N * j, N, bk, shared_w.ready[3 * q + 2],
                                 h_ready, True, True)
                wait(DVE, m, xs_done[c], x2_done[b])
                x2_done[b] = bank_free[bk] = dve.mark(DVE.scalar_tensor_tensor(
                    out=x_all[:, b, :], in0=bank[bk][0:N, :], scalar=gates[0:N, 1:2],
                    in1=x_all[:, b, :], op0=MULT, op1=ADD))
            hT_free[n % 2] = m
            if c == NCH - 1:
                shared_w.unit_free[q % NUNIT] = m

        route(0)
        pending = None
        for n, (q, c) in enumerate((q, c) for q in range(NQ) for c in range(NCH)):
            if q == 0 and c + 1 < NCH:
                table_written, counts_ready = route(c + 1)
            h_ready = gate_up_product(n, w_split[q % NUNIT], [t[:] for t in xnT[c]], CW,
                                      [shared_w.ready[3 * q], shared_w.ready[3 * q + 1]], xnT_ready[c])
            if pending:
                shared_down(*pending)
            pending = (n, q, c, h_ready)
            if c > 0:
                shared_w.split(1)
        shared_down(*pending)

        bk = next_bank()
        wait(PE, counts_ready, bank_free[bk])
        m = pe.mark(PE.matmul(bank[bk][0:N, 0:E], ones16[:], counted[:, NCH % 2, :], start=True, stop=True))
        wait(DVE, m)
        m = dve.mark(DVE.tensor_reduce(sweeps_f[:, 0:1], bank[bk][0:1, 0:E], AX.X, ALU.max))
        wait(DVE, m)
        m = dve.mark(DVE.tensor_scalar(sweep_edges[:], sweep_edges[:], sweeps_f[:, 0:1], None, ALU.is_lt))
        wait(DVE, m)
        m = dve.mark(DVE.tensor_reduce(sweeps_f[:, 1:2], sweep_edges[:], AX.X, ADD))
        wait(DVE, m)
        sweeps_ready = dve.mark(DVE.tensor_copy(sweeps[:], sweeps_f[:, 1:2]))

        for e in (PE, ACTE, DVE, POOL, SP):
            wait(e, sweeps_ready)
        wait(POOL, table_written, *rows_free, *x2_done)
        wait(SP, table_written)
        n_sweeps = nc.values_load(sweeps[0:1, 0:1], min_val=1, max_val=MAX_SWEEPS)
        loop_sems = ([counter(f"sweep_{n}") for n in "pe act dve ids y_rows0 y_rows1".split()]
                     + [counter(f"sweep_rows{i}") for i in range(4)]
                     + [counter(f"sweep_raw{i}") for i in range(NRAW)])
        nc.all_engine_barrier()
        with nc.Fori(0, n_sweeps) as sweep:
            wait = Waits()
            pe, act, dve, ids_io, *y_out = loop_sems[:6]
            rows_in, raw_in = loop_sems[6:10], loop_sems[10:]
            bank_free = [None] * 8
            hidden_free, hT_free = [None] * 2, [None] * 2
            y_free = [None] * NT
            stream = WeightStream([p for e in range(E) for q in range(NQ)
                                   for p in unit_parts(w_gate_up[e], w_down[e], q)],
                                  raw_in, wait, act, dve)
            by_sweep = lists.rearrange("(e s p i) o -> p e s (i o)", e=E, s=MAX_SWEEPS, i=NT)
            ids_ready = ids_io.mark(ACTE.dma_start(
                list_ids[:], by_sweep[:, :, bass.ds(sweep, 1), :].rearrange("p e s i -> p (e s) i")), 16)
            gathered, xsT_free, x_ready = {}, [None] * 2, {}
            rows_free = [None] * 4

            def gather(e):
                wait(POOL, ids_ready)
                for i in range(NT):
                    r = (NT * e + i) % 4
                    wait(POOL, rows_free[r])
                    gathered[e, i] = rows_in[r].mark(POOL.indirect_dma_start(
                        rows[r][:], None, gated_rows,
                        bass.IndirectOffsetOnAxis(ap=list_ids[:, e, i:i + 1], axis=0),
                        bounds_check=T - 1, oob_is_err=False), 16)

            def transpose_expert(e):
                for i in range(NT):
                    r = (NT * e + i) % 4
                    x_ready[e], rows_free[r] = transpose_rows(
                        rows[r][:], P, [t[:, :, P * i:P * i + P] for t in xnT[e % 2]], gathered[e, i],
                        xsT_free[e % 2])

            def expert_down(n, e, q, h_ready):
                for i in range(NT):
                    bk = 4 + NT * (e % 2) + i
                    m = down_product(n, w_split[n % NUNIT][2], P * i, P, bk, stream.ready[3 * n + 2],
                                     h_ready, q == 0, q == NQ - 1)
                    if q == NQ - 1:
                        wait(ACTE, m, y_free[i])
                        bank_free[bk] = copied = act.mark(ACTE.activation(y_rows[i][:], bank[bk][:], ACT.Copy))
                        wait(POOL, copied)
                        y_free[i] = y_out[i].mark(POOL.indirect_dma_start(
                            routed_rows, bass.IndirectOffsetOnAxis(ap=list_ids[:, e, i:i + 1], axis=0),
                            y_rows[i][:], None, bounds_check=T - 1, oob_is_err=False), 16)
                hT_free[n % 2] = stream.unit_free[n % NUNIT] = m

            gather(0)
            stream.split(3)
            transpose_expert(0)
            stream.split(3)
            pending = None
            for n, (e, q) in enumerate((e, q) for e in range(E) for q in range(NQ)):
                if q == 0 and e + 1 < E:
                    gather(e + 1)
                if q == NQ - 1 and e + 1 < E:
                    transpose_expert(e + 1)
                h_ready = gate_up_product(
                    n, w_split[n % NUNIT], [t[:, :, 0:SLOTS] for t in xnT[e % 2]], SLOTS,
                    [stream.ready[3 * n], stream.ready[3 * n + 1]], x_ready[e])
                if q == NQ - 1:
                    xsT_free[e % 2] = (pe, pe.value)
                if pending:
                    expert_down(*pending)
                pending = (n, e, q, h_ready)
                stream.split(3)
            expert_down(*pending)
            wait(POOL, *y_free, *[gathered[E - 2 + i // NT, i % NT] for i in range(2 * NT)])
            wait(SP, *y_free)
            nc.all_engine_barrier()
            POOL.dma_reset()
            for c in loop_sems:
                POOL.sem_clear(c.sem)
            nc.all_engine_barrier()

        wait = Waits()
        done = counter("final_done")
        final_in = [counter(f"final_in{i}") for i in range(NRAW)]
        stores = counter("stores")
        PB = 2
        free = [None] * NRAW
        routed_b = routed_rows.rearrange("(b n) d -> n b d", n=N)
        out_b = out.rearrange("b n d -> n b d")
        for n in range(B // PB):
            i, s = n % NRAW, slice(PB * n, PB * n + PB)
            dst = raw[i][0:N, :].rearrange("n (b d) -> n b d", b=PB)
            wait(SP, free[i])
            loaded = final_in[i].mark(SP.dma_start(dst, routed_b[:, s, :]), 16)
            wait(DVE, loaded)
            free[i] = m = done.mark(DVE.scalar_tensor_tensor(
                out=x_all[:, s, :], in0=dst, scalar=gates[0:N, 1:2], in1=x_all[:, s, :],
                op0=MULT, op1=ADD))
            wait(ACTE, m)
            stored = stores.mark(ACTE.dma_start(out_b[:, s, :], x_all[:, s, :]), 16)
        wait(ACTE, stored)


_INS = ["x", "ctx_2048", "g_xattn", "g_ffn", "L0_xattn_Wq", "L0_xattn_Wk", "L0_xattn_Wv",
        "L0_ffn_router_w", "L0_ffn_w_gate_up", "L0_ffn_w_down", "L0_ffn_shared_gate_up",
        "L0_ffn_shared_down"]


def kernel(**inputs):
    import numpy as np
    import concourse.bacc as bacc
    from concourse.bass_utils import run_bass_kernel_spmd

    nc = bacc.Bacc("TRN2", target_bir_lowering=False, num_devices=1)
    arrays, args = {}, []
    for name in _INS:
        arrays[name] = np.ascontiguousarray(inputs[name])
        args.append(nc.dram_tensor(name, arrays[name].shape, mybir.dt.from_np(arrays[name].dtype),
                                   kind="ExternalInput").ap())
    out = nc.dram_tensor("out", arrays["x"].shape, F32, kind="ExternalOutput").ap()
    build_program(nc, *args, out)
    result = run_bass_kernel_spmd(nc, [arrays], core_ids=[0])
    return result.results[0]["out"]
```

```python
from contextlib import ExitStack

import concourse.bass as bass
from concourse import mybir

F32 = mybir.dt.float32
F32R = mybir.dt.float32r
F16 = mybir.dt.float16
I32 = mybir.dt.int32
U32 = mybir.dt.uint32
ALU = mybir.AluOpType
ACT = mybir.ActivationFunctionType
AX = mybir.AxisListType

P = 128
LN_EPS = 1e-5
RMS_EPS = 1e-6
RSQRT_MAGIC = 0x5F3759DF


class Counter:

    def __init__(self, sem):
        self.sem, self.value = sem, 0

    def mark(self, instruction, by=1):
        instruction.then_inc(self.sem, by)
        self.value += by
        return self, self.value


class Waits:

    def __init__(self):
        self.seen = {}

    def __call__(self, engine, *marks):
        for mark in marks:
            if mark is None:
                continue
            counter, value = mark
            key = (engine.engine, counter.sem.name)
            if self.seen.get(key, 0) < value:
                engine.wait_ge(counter.sem, value)
                self.seen[key] = value


def rsqrt_step(v, wait, done, y, t, x, ready, i):
    wait(v, ready)
    if i == 0:
        return done.mark(v.tensor_scalar(y.bitcast(I32), x.bitcast(I32), -0.5, float(RSQRT_MAGIC),
                                         ALU.mult, ALU.add))
    if i % 4 == 1:
        return done.mark(v.tensor_tensor(t, y, y, ALU.mult))
    if i % 4 == 2:
        return done.mark(v.tensor_tensor(t, t, x, ALU.mult))
    if i % 4 == 3:
        return done.mark(v.tensor_scalar(t, t, -0.5, 1.5, ALU.mult, ALU.add))
    return done.mark(v.tensor_tensor(y, y, t, ALU.mult))


RSQRT_STEPS = 13
PV_LAG = 3

T_SLOTS = (-3, 2, 8, 16)
RMS_SLOTS = (1, 2, 2, 2, 2, 3, 3, 3, 4, 4, 4, 5, 5, 5)
PACK_SLOTS = (6, 8, 10, 14)
PACK_T_SLOTS = (10, 12, 14, 18)


def rsqrt_steps(nc, wait, done, y, t, x, ready):
    for i in range(RSQRT_STEPS):
        ready = rsqrt_step(nc.vector, wait, done, y, t, x, ready, i)
    return ready


def build_program(nc, x, ctx, g_xattn, g_ffn, w_q, w_k, w_v, w_router, w_gate_up, w_down,
                  w_sh_gate_up, w_sh_down, out, stage="all"):
    B, N, D = x.shape
    M = ctx.shape[1]
    HD = 16
    H = D // HD
    KD = D // P
    HPAIR = H // 2
    HROW = P // 2
    GH = 4
    NG = H // GH
    MT = [(r, min(P, M - r)) for r in range(0, M, P)]
    NMT = len(MT)
    VW = 2 * HD + 1
    SCALE = float(HD) ** -0.5
    MULT, ADD, SUB = ALU.mult, ALU.add, ALU.subtract

    stack = ExitStack()
    with stack:
        def sb(name, shape, dt, scope=None):
            return (scope or stack).enter_context(nc.sbuf_tensor(name, shape, dt))

        def counter(name):
            return Counter(stack.enter_context(nc.semaphore(name)))

        bank = [stack.enter_context(nc.psum_tensor(f"bank{i}", [P, 512], F32)) for i in range(8)]
        wait = Waits()
        pe, act, dve, pool = (counter(n) for n in ("pe_done", "act_done", "dve_done", "pool_done"))
        PE, ACTE, DVE, POOL, SP = nc.tensor, nc.scalar, nc.vector, nc.gpsimd, nc.sync

        ident32 = sb("ident32", [P, P], F32)
        ident16 = sb("ident16", [P, P], F16)
        gates = sb("gates", [P, 2], F32)
        x_all = sb("x_all", [N, B, D], F32)
        ln_stats = sb("ln_stats", [N, B, 6], F32)
        ln_mv = sb("ln_mv", [N, B, 2], F32)
        ln_var = sb("ln_var", [N, B], F32)
        ln_rstd = sb("ln_rstd", [N, B], F32)
        ln_tmp = sb("ln_tmp", [N, B], F32)

        m = pool.mark(POOL.memset(ident32[:], 0.0))
        wait(POOL, m)
        identity_ready = pool.mark(POOL.affine_select(
            out=ident32[:], in_=ident32[:], compare_op=ALU.not_equal, fill=1.0, base=0,
            pattern=[[-1, P]], channel_multiplier=1))
        wait(DVE, identity_ready)
        identity16_ready = dve.mark(DVE.tensor_copy(ident16[:], ident32[:]))

        x_in = [counter(f"x_in{i}") for i in range(4)]
        XC = B // len(x_in)

        def load_x(i):
            return x_in[i].mark(SP.dma_start(
                x_all[:, XC * i:XC * i + XC, :], x[XC * i:XC * i + XC].rearrange("b n d -> n b d")), 16)

        g_in = counter("g_in")
        for i, g in enumerate((g_xattn, g_ffn)):
            gates_loaded = g_in.mark(ACTE.dma_start(
                gates[:, i:i + 1], g.rearrange("(a n) -> a n", a=1).to_broadcast([P, 1])), 16)

        def layer_norm_stats(b0, nb, ready):
            wait(DVE, ready)
            for b in range(b0, b0 + nb):
                m = dve.mark(DVE.bn_stats(ln_stats[:, b, :], x_all[:, b, :]))
            wait(DVE, m)
            for b in range(b0, b0 + nb):
                m = dve.mark(DVE.bn_aggr(ln_mv[:, b, :], ln_stats[:, b, :]))
            wait(DVE, m)
            s = slice(b0, b0 + nb)
            m = dve.mark(DVE.tensor_scalar(ln_var[:, s], ln_mv[:, s, 1], LN_EPS, None, ADD))
            return rsqrt_steps(nc, wait, dve, ln_rstd[:, s], ln_tmp[:, s], ln_var[:, s], m)

        bank_free = [None] * 8
        x1_done = [None] * B
        arena_f32r = sb("arena_f32r", [P, 2 * 3 * KD * D + 2 * 2 * KD * P + 32], F32R)
        arena_f32 = sb("arena_f32", [P, (5 + 1 + 1 + NMT + 1) * D], F32)
        rstd_ready = [None] * (B // XC)
        moe = feed_forward(locals())
        moe_at = [None]
        attention(locals())
        if stage == "x1":
            st = counter("stores")
            wait(SP, *x1_done)
            s = st.mark(SP.dma_start(out.rearrange("b n d -> n b d"), x_all[:]), 16)
            wait(SP, s)
            return
        while moe_at[0] != "attention over":
            moe_at[0] = next(moe)
        nc.all_engine_barrier()
        for _ in moe:
            pass


def carver(arena):
    offset = 0

    def carve(rows, shape, dt):
        nonlocal offset
        count = 1
        for n in shape:
            count *= n
        words = -(-count * mybir.dt.size(dt) // 4)
        view = arena[0:rows, offset:offset + words]
        offset += words
        assert offset <= arena.shape[1]
        if dt != arena.dtype:
            view = view.bitcast(dt)[:, 0:count]
        if len(shape) == 1:
            return view
        names = " ".join("abcd"[:len(shape)])
        return view.rearrange(f"p ({names}) -> p {names}", **dict(zip("abcd", shape)))

    return carve


def attention(env):
    (nc, stack, sb, counter, bank, wait, pe, act, dve, pool, PE, ACTE, DVE, POOL, SP, B, N, D, M, HD,
     H, KD, HPAIR, HROW, GH, NG, MT, NMT, VW, SCALE, MULT, ADD, SUB) = (env[k] for k in (
        "nc stack sb counter bank wait pe act dve pool PE ACTE DVE POOL SP B N D M HD H KD HPAIR "
        "HROW GH NG MT NMT VW SCALE MULT ADD SUB").split())
    ident32, ident16, identity_ready, identity16_ready = (
        env[k] for k in "ident32 ident16 identity_ready identity16_ready".split())
    x_all, ln_mv, ln_rstd, gates, gates_loaded, load_x, XC, x1_done, ctx = (
        env[k] for k in "x_all ln_mv ln_rstd gates gates_loaded load_x XC x1_done ctx".split())
    scope = ExitStack()
    with scope:
        def buf(name, shape, dt):
            return sb(name, shape, dt, scope)

        carve_f32r, carve = carver(env["arena_f32r"]), carver(env["arena_f32"])
        wqT = [carve_f32r(P, [KD, D], F32R) for _ in range(2)]
        wkvT = [carve_f32r(P, [KD, 2, D], F32R) for _ in range(2)]
        NRAW = 5
        raw = [carve(P, [D], F32) for i in range(NRAW)]
        raw_in = [counter(f"raw_in{i}") for i in range(NRAW)]
        raw_free = [None] * NRAW
        srcT = [[carve_f32r(P, [KD, P], F32R) for _ in range(2)] for i in range(2)]
        xn = carve(N, [D], F32)
        square = carve(P, [D], F32)
        k_raw = carve(P, [NMT, D], F32)
        q_raw = carve(N, [D], F32)
        sumsq = [buf(f"sumsq{i}", [P, NMT + 1, H], F32) for i in range(2)]
        rms = [buf(f"rms{i}", [P, NMT + 1, H], F32) for i in range(2)]
        rms_tmp = buf("rms_tmp", [P, NMT + 1, H], F32)
        normed = [buf(f"normed{i}", [P, D], F32) for i in range(2)]
        k_pack = [buf(f"k_pack{t}", [P, H, HROW], F16) for t in range(NMT)]
        q_pack = buf("q_pack", [N, H, HROW], F16)
        kT = [buf(f"kT{i}", [P, HPAIR, NMT * P], F16) for i in range(2)]
        qT = [buf(f"qT{i}", [P, HPAIR, 2 * N], F16) for i in range(2)]
        v_pack = [buf(f"v_pack{i}", [P, NMT, H, VW], F16) for i in range(3)]
        NPR = 2
        probs = [buf(f"probs{i}", [P, 2, GH, N], F32) for i in range(NPR)]
        probs_hi = [buf(f"probs_hi{i}", [P, 2, GH, P], F16) for i in range(NPR)]
        probs_lo = [buf(f"probs_lo{i}", [P, 2, GH, P], F16) for i in range(NPR)]
        heads_out = buf("heads_out", [N, H, VW], F32)
        inv_sum = buf("inv_sum", [N, H], F32)

        for t in v_pack:
            m = pool.mark(POOL.memset(t[:, :, :, HD:HD + 1], 1.0))
        for t in sumsq:
            m = pool.mark(POOL.memset(t[:], 1.0))
        for t in k_pack + [q_pack] + qT + probs_hi + probs_lo:
            m = pool.mark(POOL.memset(t[:].bitcast(F32), 0.0))
        constants_ready = m

        bank_free = env["bank_free"]

        n_raw = 0

        def load_rows(src):
            nonlocal n_raw
            i = n_raw % NRAW
            n_raw += 1
            wait(SP, raw_free[i])
            ready = raw_in[i].mark(SP.dma_start(raw[i][0:src.shape[0], :], src), 16)
            return i, ready

        ctx_tiles = [(b, t) for b in range(B) for t in range(NMT)]
        ctx_loaded = {}

        def prefetch_ctx():
            if len(ctx_loaded) < len(ctx_tiles):
                b, t = ctx_tiles[len(ctx_loaded)]
                r, m = MT[t]
                ctx_loaded[b, t] = load_rows(ctx[b, r:r + m, :])

        weights = [(w, j) for w in ("w_k", "w_v", "w_q") for j in range(KD)]
        early = 2 * KD
        w_loaded, w_turned = [], [None] * len(weights)
        w_bank = [(0, 2, 3, 4, 5, 6)[n % 6] for n in range(early)] + [4, 5, 6, 7]

        def load_weight():
            if len(w_loaded) < len(weights):
                w, j = weights[len(w_loaded)]
                w_loaded.append(load_rows(env[w][P * j:P * j + P, :]))
            else:
                prefetch_ctx()

        def weight_views(n):
            w, j = weights[n]
            if w == "w_q":
                src = bank[w_bank[n]][:].rearrange("p (k c) -> p k c", k=KD)
                return src, *(t[:, :, P * j:P * j + P] for t in wqT)
            src = bank[w_bank[n]][:].rearrange("p (k c s) -> p k s c", k=KD, s=2)
            c0 = (D // 2 if w == "w_v" else 0) + P // 2 * j
            return src, *(t[:, :, :, c0:c0 + P // 2] for t in wkvT)

        def weight_on_pe(n):
            i, ready = w_loaded[n]
            bk = w_bank[n]
            wait(PE, ready, bank_free[bk])
            for k in range(KD):
                tr = PE.transpose(bank[bk][:, P * k:P * k + P], raw[i][:, P * k:P * k + P], ident32[:])
            raw_free[i] = w_turned[n] = pe.mark(tr)
            load_weight()

        def weight_on_act(n):
            src, hi, lo = weight_views(n)
            wait(ACTE, w_turned[n])
            w_turned[n] = act.mark(ACTE.activation(hi, src, ACT.Copy))

        def weight_on_dve(n):
            src, hi, lo = weight_views(n)
            wait(DVE, w_turned[n])
            w_turned[n] = bank_free[w_bank[n]] = dve.mark(
                DVE.tensor_tensor(lo, src, hi.bitcast(F32), SUB))

        for _ in range(NRAW):
            load_weight()
        wait(PE, identity_ready)
        for n in range(early):
            weight_on_pe(n)
            weight_on_act(n)
            weight_on_dve(n)

        units = [(g, t) for g in range(NG) for t in range(NMT)]
        SLOTS = len(units)
        agenda = {}

        def at(slot, engine, step, *args):
            agenda.setdefault((slot, engine), []).append((step, args))

        mark = {}
        prj_ring, tr_ring = [0], [0]

        def next_prj_bank():
            prj_ring[0] += 1
            return (2, 3)[prj_ring[0] % 2]

        def next_tr_bank():
            tr_ring[0] += 1
            return (0, 1)[tr_ring[0] % 2]

        def transpose_source(slot, b, t):
            side = t % 2
            rows = MT[t][1] if t < NMT else N

            def on_pe():
                if t < NMT:
                    i, ready = ctx_loaded[b, t]
                    src = raw[i][0:rows, :]
                else:
                    src, ready = xn[:], mark["xn", b]
                bk = mark["bank", b, t] = next_tr_bank()
                wait(PE, ready, bank_free[bk])
                for k in range(KD):
                    tr = PE.transpose(bank[bk][:, P * k:P * k + rows], src[:, P * k:P * k + P],
                                      ident32[0:rows, 0:rows])
                mark["T", b, t] = transposed = pe.mark(tr)
                if t < NMT:
                    raw_free[i] = transposed
                    prefetch_ctx()
                else:
                    mark["xn free"] = transposed

            def views():
                psum = bank[mark["bank", b, t]][:].rearrange("p (k r) -> p k r", k=KD)[:, :, 0:rows]
                return psum, *(s[:, :, 0:rows] for s in srcT[side])

            def on_act():
                psum, hi, lo = views()
                wait(ACTE, mark["T", b, t], mark.get(("src free", side)))
                mark["src high", b, t] = act.mark(ACTE.activation(hi, psum, ACT.Copy))

            def on_dve():
                psum, hi, lo = views()
                wait(DVE, mark["src high", b, t])
                mark["src", b, t] = bank_free[mark["bank", b, t]] = dve.mark(
                    DVE.tensor_tensor(lo, psum, hi.bitcast(F32), SUB))

            at(slot, "pe", on_pe)
            at(slot + 1, "act", on_act)
            at(slot + 2, "dve", on_dve)

        def project(slots, b, t, weight):
            side = t % 2
            rows = MT[t][1] if t < NMT else N
            name = "prj", b, t, weight
            w = {"q": wqT, "k": [a[:, :, 0, :] for a in wkvT], "v": [a[:, :, 1, :] for a in wkvT]}[weight]
            products = [(k, a, c) for k in range(KD) for a, c in ((0, 0), (0, 1), (1, 0))]

            def on_pe(n):
                k, a, c = products[n]
                if n == 0:
                    mark["bank", name] = bk = next_prj_bank()
                    wait(PE, mark["src", b, t], bank_free[bk])
                mm = PE.matmul(bank[mark["bank", name]][0:rows, :], srcT[side][a][:, k, 0:rows],
                               w[c][:, k], start=(n == 0), stop=(n == len(products) - 1))
                if n == len(products) - 1:
                    mark[name] = mark["src free", side] = pe.mark(mm)

            for n, slot in enumerate(slots):
                at(slot, "pe", on_pe, n)

        def take_heads(slot, b, t, weight):
            rows, dst = (MT[t][1], k_raw[0:MT[t][1], t, :]) if t < NMT else (N, q_raw[:])
            name = "prj", b, t, weight

            def copy():
                wait(ACTE, mark[name], mark.get(("scaled", b - 1, t)))
                mark["raw", b, t] = act.mark(ACTE.activation(
                    dst, bank[mark["bank", name]][0:rows, :], ACT.Copy))

            def take_square():
                wait(ACTE, mark.get("square free"))
                mark["square"] = bank_free[mark["bank", name]] = act.mark(ACTE.activation(
                    square[0:rows, :], bank[mark["bank", name]][0:rows, :], ACT.Square))

            def reduce():
                wait(DVE, mark["square"], mark.get(("rms", b - 2)))
                mark["sumsq", b, t] = mark["square free"] = dve.mark(DVE.tensor_reduce(
                    sumsq[b % 2][0:rows, t, :],
                    square[0:rows, :].rearrange("p (h d) -> p h d", d=HD), AX.X, ADD))

            at(slot, "act", copy)
            at(slot, "act", take_square)
            at(slot + 1, "dve", reduce)

        def take_values(slot, b, t):
            name = "prj", b, t, "v"
            m = MT[t][1]
            vp = v_pack[b % 3][0:m, t]

            def psum():
                return bank[mark["bank", name]][0:m, :].rearrange("p (h d) -> p h d", d=HD)

            def on_act():
                wait(ACTE, mark[name], mark.get(("values", b - 3)))
                mark["v high", b, t] = act.mark(ACTE.activation(vp[:, :, 0:HD], psum(), ACT.Copy))

            def on_dve():
                wait(DVE, mark["v high", b, t])
                mark["v", b] = bank_free[mark["bank", name]] = dve.mark(
                    DVE.tensor_tensor(vp[:, :, HD + 1:VW], psum(), vp[:, :, 0:HD], SUB))

            at(slot, "act", on_act)
            at(slot + 1, "dve", on_dve)

        def normalise_x(slot, b):
            def on_dve():
                wait(DVE, mark["stats", b // XC], mark.get("xn free"))
                mark["xn", b] = dve.mark(DVE.tensor_scalar(
                    xn[:], x_all[:, b, :], ln_mv[:, b, 0:1], ln_rstd[:, b:b + 1], SUB, MULT))
            at(slot, "dve", on_dve)

        def rms_factors(slots, b):
            s = sumsq[b % 2][:]

            def mean():
                wait(DVE, *[mark["sumsq", b, t] for t in range(NMT + 1)],
                     mark.get(("scaled", b - 2, NMT)))
                mark["rms", b] = dve.mark(DVE.tensor_scalar(s, s, 1.0 / HD, RMS_EPS, MULT, ADD))

            def step(i):
                engine, done = (DVE, dve) if i == 0 else (POOL, pool)
                mark["rms", b] = rsqrt_step(engine, wait, done, rms[b % 2][:], rms_tmp[:], s,
                                            mark["rms", b], i)

            at(slots[0], "dve", mean)
            for i, slot in enumerate(slots[1:]):
                at(slot, "dve" if i == 0 else "pool", step, i)

        def make_pack(slot, b, t):
            if t < NMT:
                rows, src, pack, places, low_place = MT[t][1], k_raw[:, t, :], k_pack[t], (0, 2 * HD), HD
            else:
                rows, src, pack, places, low_place = N, q_raw[:], q_pack, (0, HD), 2 * HD
            n = normed[t % 2][0:rows, :]
            nh = n.rearrange("p (h d) -> p h d", d=HD)

            def scale():
                wait(DVE, mark["rms", b], mark["raw", b, t], mark.get(("normed free", t % 2)))
                mark["scaled", b, t] = dve.mark(DVE.tensor_tensor(
                    nh, src[0:rows].rearrange("p (h d) -> p h d", d=HD),
                    rms[b % 2][0:rows, t, :].unsqueeze(2).to_broadcast([rows, H, HD]), MULT))

            def high():
                a, c = places
                wide = pack[0:rows, :, a:c + HD].rearrange(
                    "p h (s d) -> p h s d", d=HD)[:, :, ::(c - a) // HD, :]
                wait(ACTE, mark["scaled", b, t], mark.get(("pack transposed", b - 1, t)))
                mark["pack high", b, t] = act.mark(ACTE.activation(
                    wide, nh.unsqueeze(2).to_broadcast([rows, H, 2, HD]), ACT.Copy))

            def low():
                wait(POOL, mark["pack high", b, t])
                mark["pack", b, t] = mark["normed free", t % 2] = pool.mark(POOL.tensor_tensor(
                    pack[0:rows, :, low_place:low_place + HD], nh,
                    pack[0:rows, :, places[0]:places[0] + HD], SUB))

            at(slot, "dve", scale)
            at(slot + 1, "act", high)
            at(slot + 2, "pool", low)

        def transpose_pack(slot, b, t, half):
            pack, rows = (k_pack[t], P) if t < NMT else (q_pack, N)
            name = "bank", "pack", b, t, half
            pairs = slice(HPAIR // 2 * half, HPAIR // 2 * (half + 1))

            def psum():
                return bank[mark[name]][:].bitcast(F16).rearrange("p (a r) -> p a r", a=HPAIR // 2)

            def on_pe():
                bk = mark[name] = next_tr_bank()
                wait(PE, mark["pack", b, t], bank_free[bk])
                for a in range(HPAIR // 2):
                    pair = HPAIR // 2 * half + a
                    tr = PE.transpose(psum()[:, a, 0:rows], pack[0:rows, 2 * pair:2 * pair + 2, :]
                                      .rearrange("p a c -> p (a c)"), ident16[0:rows, 0:rows])
                mark["pack transposed", b, t] = mark["pack T", b, t, half] = pe.mark(tr)

            def on_act():
                wait(ACTE, mark["pack T", b, t, half], mark.get(("scored", b - 2)))
                if t < NMT:
                    m = act.mark(ACTE.activation(
                        kT[b % 2][:, pairs, P * t:P * t + P].bitcast(F32), psum().bitcast(F32), ACT.Copy))
                else:
                    for z in range(2):
                        rows_z = slice(HROW * z, HROW * z + HROW)
                        m = act.mark(ACTE.activation(
                            qT[b % 2][rows_z, pairs, N * z:N * z + N].bitcast(F32),
                            psum()[rows_z, :, 0:N].bitcast(F32), ACT.Copy))
                mark["kT", b] = bank_free[mark[name]] = m

            at(slot, "pe", on_pe)
            at(slot + 1, "act", on_act)

        def unit(s):
            return (s // SLOTS, *units[s % SLOTS]) if 0 <= s < B * SLOTS else None

        sc_banks, pv_banks = (4, 5), (6, 7)

        def scores(s):
            b, g, t = unit(s)
            bk = sc_banks[s % 2]
            wait(PE, mark["kT", b], bank_free[bk])
            for a in range(GH // 2):
                pair = GH // 2 * g + a
                mm = PE.matmul(bank[bk][:, 2 * N * a:2 * N * (a + 1)],
                               kT[b % 2][:, pair, P * t:P * t + P], qT[b % 2][:, pair, :],
                               start=True, stop=True)
            mark["scored", b] = mark["scores", s % 2] = pe.mark(mm)

        def exp_scores(s):
            bk = sc_banks[s % 2]
            i = s // 2 % NPR
            wait(ACTE, mark["scores", s % 2], mark.get(("probs free", i)))
            mark["probs", i] = bank_free[bk] = act.mark(ACTE.activation(
                probs[i][:, s % 2], bank[bk][:, 0:GH * N].rearrange("p (h n) -> p h n", h=GH),
                ACT.Exp, scale=SCALE))

        def split_high(s):
            i = (s - 2) // 2 % NPR
            wait(DVE, mark["probs", i], mark.get(("split free", i)))
            mark["high", i] = dve.mark(DVE.tensor_copy(probs_hi[i][:, :, :, 0:N], probs[i][:]))

        def split_low(s):
            i = (s - 2) // 2 % NPR
            wait(DVE, mark["high", i])
            mark["split", i] = mark["probs free", i] = dve.mark(DVE.tensor_tensor(
                probs_lo[i][:, :, :, 0:N], probs[i][:], probs_hi[i][:, :, :, 0:N], SUB))

        def weighted_values(s):
            b, g, t = unit(s)
            bk = pv_banks[g % 2]
            m = MT[t][1]
            i = s // 2 % NPR
            wait(PE, mark["split", i], mark["v", b], bank_free[bk])
            for h in range(GH):
                v = v_pack[b % 3][0:m, t, GH * g + h, :]
                col = VW * h
                PE.matmul(bank[bk][:, col:col + VW], probs_hi[i][0:m, s % 2, h, :], v,
                          start=(t == 0 and h == 0), stop=False, skip_group_check=True)
                mm = PE.matmul(bank[bk][:, col:col + HD + 1], probs_lo[i][0:m, s % 2, h, :], v[:, 0:HD + 1],
                               start=False, stop=(t == NMT - 1 and h == GH - 1),
                               skip_group_check=True)
            mark["split free", i] = mark["values", b] = pe.mark(mm)

        def take_outputs(b, g, heads_free):
            bk = pv_banks[g % 2]
            wait(ACTE, mark["values", b], heads_free())
            mark["heads", b] = bank_free[bk] = act.mark(ACTE.activation(
                heads_out[:, GH * g:GH * g + GH, :],
                bank[bk][0:N, 0:GH * VW].rearrange("p (h c) -> p h c", h=GH), ACT.Copy))

        def finish_attention(slot, b):
            o = heads_out[:, :, 0:HD]
            xb = x_all[:, b, :].rearrange("p (h d) -> p h d", d=HD)

            def invert():
                wait(DVE, mark["heads", b], mark["gates"])
                mark["inv"] = dve.mark(DVE.reciprocal(inv_sum[:], heads_out[:, :, HD]))

            def add_parts():
                mark["o"] = dve.mark(DVE.tensor_tensor(o, heads_out[:, :, 0:HD],
                                                       heads_out[:, :, HD + 1:VW], ADD))

            def divide():
                wait(DVE, mark["inv"], mark["o"])
                mark["o"] = dve.mark(DVE.tensor_tensor(
                    o, o, inv_sum[:].unsqueeze(2).to_broadcast([N, H, HD]), MULT))

            def add_to_x():
                wait(DVE, mark["o"])
                x1_done[b] = mark["x1", b] = dve.mark(DVE.scalar_tensor_tensor(
                    out=xb, in0=o, scalar=gates[0:N, 0:1], in1=xb, op0=MULT, op1=ADD))

            at(slot, "dve", invert)
            at(slot, "dve", add_parts)
            at(slot + 1, "dve", divide)
            at(slot + 1, "dve", add_to_x)

        PJ = 3 * KD
        projections = [(t, w) for t in range(NMT) for w in ("v", "k")] + [(NMT, "q")]
        pj_slots = [n * SLOTS // (PJ * len(projections)) for n in range(PJ * len(projections))]
        for j in range(KD):
            at(-2 * SLOTS + T_SLOTS[0] - KD + j, "pe", weight_on_pe, early + j)
            at(-2 * SLOTS + T_SLOTS[0] - KD + j + 1, "act", weight_on_act, early + j)
            at(-2 * SLOTS + T_SLOTS[0] - KD + j + 2, "dve", weight_on_dve, early + j)
        def request_x(i):
            mark["x", i] = load_x(i)

        def x_stats(i):
            mark["stats", i] = env["layer_norm_stats"](XC * i, XC, mark["x", i])

        def gate_factors():
            wait(ACTE, gates_loaded)
            mark["gates"] = act.mark(ACTE.activation(gates[:], gates[:], ACT.Tanh))

        at(-SLOTS, "act", gate_factors)
        for i in range(B // XC):
            at(-2 * SLOTS + 2 + 4 * i, "pe", request_x, i)
            at(-2 * SLOTS + 10 + 7 * i, "dve", x_stats, i)
        for b in range(-2, B):
            w0 = SLOTS * b
            c, d = b + 1, b + 2
            if d < B:
                for t, slot in zip(range(NMT + 1), T_SLOTS):
                    transpose_source(w0 + slot, d, t)
                normalise_x(w0 + T_SLOTS[NMT] - 2, d)
                for i, (t, weight) in enumerate(projections):
                    slots = pj_slots[PJ * i:PJ * i + PJ]
                    project([w0 + s for s in slots], d, t, weight)
                    if weight == "v":
                        take_values(w0 + slots[-1] + 1, d, t)
                    else:
                        take_heads(w0 + slots[-1] + 1, d, t, weight)
                rms_factors([w0 + SLOTS + s for s in RMS_SLOTS], d)
            if 0 <= c < B:
                for t in range(NMT + 1):
                    make_pack(w0 + PACK_SLOTS[t], c, t)
                    for half in range(2):
                        transpose_pack(w0 + PACK_T_SLOTS[t] + half, c, t, half)
            if b >= 0:
                for g in range(NG):
                    at(w0 + NMT * g + NMT - 1 + PV_LAG + 1, "act", take_outputs, b, g,
                       lambda b=b: mark.get(("x1", b - 1)))
                finish_attention(w0 + SLOTS + PV_LAG + 1, b)

        def x1_stats(b):
            wait(DVE, x1_done[b])
            m = dve.mark(DVE.bn_stats(env["ln_stats"][:, b, :], x_all[:, b, :]))
            wait(DVE, m)
            mark["x1 mv", b] = dve.mark(DVE.bn_aggr(ln_mv[:, b, :], env["ln_stats"][:, b, :]))

        def x1_var(c):
            ch = slice(XC * c, XC * c + XC)
            wait(DVE, *[mark["x1 mv", b] for b in range(XC * c, XC * c + XC)])
            mark["x1 rstd", c] = dve.mark(DVE.tensor_scalar(
                env["ln_var"][:, ch], ln_mv[:, ch, 1], LN_EPS, None, ADD))

        def x1_rstd(c, i):
            ch = slice(XC * c, XC * c + XC)
            engine, done = (DVE, dve) if i == 0 else (POOL, pool)
            mark["x1 rstd", c] = env["rstd_ready"][c] = rsqrt_step(
                engine, wait, done, ln_rstd[:, ch], env["ln_tmp"][:, ch], env["ln_var"][:, ch],
                mark["x1 rstd", c], i)

        moe, moe_at = env["moe"], env["moe_at"]
        for b in range(B):
            at(SLOTS * (b + 1) + PV_LAG + 3, "dve", x1_stats, b)
        for c in range(B // XC):
            s0 = SLOTS * XC * (c + 1) + PV_LAG + 4
            at(s0, "dve", x1_var, c)
            for i in range(RSQRT_STEPS):
                at(s0 + 1 + i // 2, "dve" if i == 0 else "pool", x1_rstd, c, i)

        def early_feed_forward():
            if moe_at[0] != "attention over":
                moe_at[0] = next(moe)

        def free_arena():
            next(moe)
            moe.send((mark["prj", B - 1, NMT, "q"], mark["square free"], mark["scaled", B - 1, NMT]))

        s0 = SLOTS * (B - 2) + PACK_SLOTS[NMT] + 1
        at(s0, "pe", free_arena)
        for slot in range(s0 + 1, SLOTS * B):
            at(slot, "pe", early_feed_forward)

        wait(PE, w_turned[early - 1], identity16_ready)
        wait(ACTE, constants_ready)
        wait(DVE, constants_ready)
        for s in range(min(slot for slot, _ in agenda), max(slot for slot, _ in agenda) + 1):
            if unit(s + 1):
                scores(s + 1)
            if unit(s):
                exp_scores(s)
            for step, args in agenda.get((s, "act"), []):
                step(*args)
            fills = agenda.get((s, "dve"), [])
            own = [(split_high if s % 2 == 0 else split_low, (s,))] if unit(s - 2) else []
            for i in range(max(len(fills), len(own))):
                for step, args in own[i:i + 1] + fills[i:i + 1]:
                    step(*args)
            for step, args in agenda.get((s, "pool"), []) + agenda.get((s, "pe"), []):
                step(*args)
            if unit(s - PV_LAG):
                weighted_values(s - PV_LAG)


def feed_forward(env):
    (nc, stack, sb, counter, bank, PE, ACTE, DVE, POOL, SP, B, N, D, KD, MULT, ADD, SUB) = (
        env[k] for k in "nc stack sb counter bank PE ACTE DVE POOL SP B N D KD MULT ADD SUB".split())
    wait, pe, act, dve, pool, bank_free = (env[k] for k in "wait pe act dve pool bank_free".split())
    ident32, x_all, gates, out = (env[k] for k in "ident32 x_all gates out".split())
    ln_stats, ln_mv, ln_var, ln_rstd, ln_tmp = (
        env[k] for k in "ln_stats ln_mv ln_var ln_rstd ln_tmp".split())
    rstd_ready = env["rstd_ready"]
    w_router, w_gate_up, w_down, w_sh_gate_up, w_sh_down = (
        env[k] for k in "w_router w_gate_up w_down w_sh_gate_up w_sh_down".split())
    E, F = w_down.shape[0], w_down.shape[1]
    T = B * N
    CT = 4
    NCH = B // CT
    CW = CT * N
    FQ = 256
    NQ = F // FQ
    KF = FQ // P
    SLOTS = 2 * P
    MAX_SWEEPS = -(-T // SLOTS)
    CAP = MAX_SWEEPS * SLOTS
    NT = SLOTS // P

    gated_rows = nc.dram_tensor("gated_rows", (T, D), F32).ap()
    routed_rows = nc.dram_tensor("routed_rows", (T, D), F32).ap()
    lists = nc.dram_tensor("expert_lists", (E * CAP, 1), I32).ap()

    scope = ExitStack()
    with scope:
        def buf(name, shape, dt):
            return sb(name, shape, dt, scope)

        carve_f32r, carve = carver(env["arena_f32r"]), carver(env["arena_f32"])
        NRAW = 4
        PART = KD * FQ
        raw = [carve(P, [PART], F32) for i in range(2)]
        w_split = [[[carve_f32r(P, [PART], F32R) for _ in range(2)] for _ in range(3)]]
        xnT = [[carve_f32r(P, [KD, CW], F32R) for _ in range(2)] for _ in range(2)]
        wrT = [carve_f32r(P, [KD, P], F32R) for _ in range(2)]
        rows = [carve(P, [D], F32) for i in range(4)]
        logitsT = carve(E, [CW], F32)
        logits = carve(N, [CT, E], F32)
        top = carve(N, [CT, E], F32)
        top_index = carve(N, [CT, E], U32)
        expert = carve(N, [CT], F32)
        gate = carve(N, [CT], F32)
        gate_rstd = carve(N, [CT], F32)
        onehot = carve(N, [CT, E], F16)
        counted = carve(N, [2, E], F16)
        chunk_count = carve(N, [E], F32)
        place = carve(N, [CT, E], F32)
        slot_f = carve(N, [CT], F32)
        slot = carve(N, [B], I32)
        token_id = carve(N, [B], I32)
        columns = carve(N, [E], F32)
        list_base = carve(N, [E], F32)
        before = carve(N, [N], F16)
        ones16 = carve(N, [N], F16)
        sweep_edges = carve(1, [MAX_SWEEPS], F32)
        sweeps_f = carve(1, [2], F32)
        sweeps = carve(1, [1], I32)
        none_fill = carve(P, [E * CAP // P], I32)
        list_ids = carve(P, [E, NT], I32)

        arena_free = yield
        for engine in (SP, ACTE, DVE, POOL):
            wait(engine, *arena_free)

        m = pool.mark(POOL.iota(token_id[:], [[N, B]], base=0, channel_multiplier=1))
        m = pool.mark(POOL.iota(columns[:], [[1, E]], base=0, channel_multiplier=0,
                                allow_small_or_imprecise_dtypes=True))
        m = pool.mark(POOL.iota(list_base[:], [[CAP, E]], base=0, channel_multiplier=0,
                                allow_small_or_imprecise_dtypes=True))
        m = pool.mark(POOL.iota(sweep_edges[:], [[SLOTS, MAX_SWEEPS]], base=0, channel_multiplier=0,
                                allow_small_or_imprecise_dtypes=True))
        m = pool.mark(POOL.iota(none_fill[:], [[0, E * CAP // P]], base=T, channel_multiplier=0))
        filled = m
        POOL.memset(ones16[:], 1.0)
        POOL.memset(counted[:], 0.0)
        for t in rows:
            m = pool.mark(POOL.memset(t[:], 0.0))
        wait(POOL, m)
        m = pool.mark(POOL.affine_select(out=before[:], in_=ones16[:], compare_op=ALU.is_gt, fill=0.0,
                                         base=0, pattern=[[1, N]], channel_multiplier=-1))
        constants_ready = m
        lists_io = counter("lists_io")
        wait(POOL, filled)
        lists_cleared = lists_io.mark(POOL.dma_start(
            lists.rearrange("(p c) o -> p (c o)", p=P), none_fill[:]), 16)
        yield

        NUNIT = 1

        def unit_parts(gate_up, down, q):
            g = gate_up.rearrange("(k p) f -> p k f", p=P)
            d = down.rearrange("(k p) n -> p k n", p=P)
            return [g[:, :, FQ * q:FQ * q + FQ], g[:, :, F + FQ * q:F + FQ * q + FQ],
                    d[:, KF * q:KF * q + KF, :]]

        class WeightStream:

            def __init__(self, parts, raw_in, wait, act, dve):
                self.parts, self.raw_in = parts, raw_in
                self.wait, self.act, self.dve = wait, act, dve
                self.loaded, self.n_split = [], 0
                self.raw_free = [None] * NRAW
                self.unit_free = [None] * 3
                self.ready = {}
                self.load(len(raw))

            def load(self, n):
                for part in self.parts[len(self.loaded):len(self.loaded) + n]:
                    i = len(self.loaded) % NRAW
                    self.wait(SP, self.raw_free[i])
                    dst = raw[i][:].rearrange("p (a c) -> p a c", a=part.shape[1])
                    self.loaded.append(self.raw_in[i].mark(SP.dma_start(dst, part), 16))

            def split(self, n, reload=True):
                for _ in range(min(n, len(self.parts) - self.n_split)):
                    part = self.n_split
                    self.n_split += 1
                    i = part % NRAW
                    u, which = divmod(part, 3)
                    hi, lo = w_split[u % NUNIT][which]
                    self.wait(ACTE, self.loaded[part], self.unit_free[u % NUNIT])
                    high = self.act.mark(ACTE.activation(hi[:], raw[i][:], ACT.Copy))
                    self.wait(DVE, high)
                    low = self.dve.mark(DVE.tensor_tensor(lo[:], raw[i][:], hi[:].bitcast(F32), SUB))
                    self.raw_free[i] = self.ready[part] = low
                    if reload:
                        self.load(1)

        raw_in = [counter(f"w_raw_in{i}") for i in range(NRAW)]
        shared_w = WeightStream([p for q in range(NQ) for p in unit_parts(w_sh_gate_up, w_sh_down, q)],
                                raw_in, wait, act, dve)
        n_bank = 0
        ring = (2, 3)

        def next_bank():
            nonlocal n_bank
            n_bank += 1
            return ring[n_bank % len(ring)]

        def transpose_rows(src, n_rows, dst, ready, dst_free=None):
            bk = next_bank()
            wait(PE, ready, bank_free[bk])
            for k in range(KD):
                tr = PE.transpose(bank[bk][:, P * k:P * k + n_rows], src[:, P * k:P * k + P],
                                  ident32[0:n_rows, 0:n_rows])
            transposed = pe.mark(tr)
            psum = bank[bk][:].rearrange("p (k r) -> p k r", k=KD)[:, :, 0:n_rows]
            wait(ACTE, transposed, dst_free)
            high = act.mark(ACTE.activation(dst[0], psum, ACT.Copy))
            wait(DVE, high)
            low = dve.mark(DVE.tensor_tensor(dst[1], psum, dst[0].bitcast(F32), SUB))
            bank_free[bk] = low
            return low, transposed

        router_in = counter("router_in")
        wait(SP, constants_ready)
        router_loaded = router_in.mark(SP.dma_start(rows[0][0:E, :], w_router), 16)
        wait(DVE, constants_ready)
        for t in wrT:
            m = dve.mark(DVE.tensor_copy(t[:], rows[1][:].rearrange("p (k c) -> p k c", k=KD)))
        yield
        router_ready, transposed = transpose_rows(rows[0][0:E, :], E, [t[:, :, 0:E] for t in wrT],
                                                  router_loaded, m)
        rows_free = [transposed, None, None, None]
        n_rows = 0
        wait(PE, constants_ready)
        yield

        rows_out = [counter(f"rows_out{i}") for i in range(4)]
        table_io = counter("table_io")
        xnT_ready = [None] * NCH
        xs_done = [None] * NCH
        small_free = {}

        def next_rows():
            nonlocal n_rows
            n_rows += 1
            return (n_rows - 1) % 4

        def route(c):
            b0 = CT * c
            s = slice(b0, b0 + CT)
            r, bk = [None] * CT, [None] * CT
            normal, transposed, high = [None] * CT, [None] * CT, [None] * CT
            for step in range(CT + 3):
                j = step
                if j < CT:
                    r[j] = i = next_rows()
                    wait(DVE, rstd_ready[c], rows_free[i])
                    normal[j] = dve.mark(DVE.tensor_scalar(
                        rows[i][0:N, :], x_all[:, b0 + j, :], ln_mv[:, b0 + j, 0:1],
                        ln_rstd[:, b0 + j:b0 + j + 1], SUB, MULT))
                j = step - 3
                if 0 <= j < CT:
                    psum = bank[bk[j]][:].rearrange("p (k r) -> p k r", k=KD)[:, :, 0:N]
                    hi, lo = (t[:, :, N * j:N * j + N] for t in xnT[c])
                    wait(DVE, high[j])
                    xnT_ready[c] = bank_free[bk[j]] = dve.mark(
                        DVE.tensor_tensor(lo, psum, hi.bitcast(F32), SUB))
                j = step - 2
                if 0 <= j < CT:
                    psum = bank[bk[j]][:].rearrange("p (k r) -> p k r", k=KD)[:, :, 0:N]
                    wait(ACTE, transposed[j])
                    high[j] = act.mark(ACTE.activation(xnT[c][0][:, :, N * j:N * j + N], psum, ACT.Copy))
                j = step - 1
                if 0 <= j < CT:
                    bk[j] = next_bank()
                    wait(PE, normal[j], bank_free[bk[j]])
                    for k in range(KD):
                        tr = PE.transpose(bank[bk[j]][:, P * k:P * k + N],
                                          rows[r[j]][0:N, P * k:P * k + P], ident32[0:N, 0:N])
                    transposed[j] = rows_free[r[j]] = pe.mark(tr)
                yield
            bk = next_bank()
            wait(PE, xnT_ready[c], router_ready, bank_free[bk])
            for k in range(KD):
                for n, (a, x) in enumerate(((0, 0), (0, 1), (1, 0))):
                    mm = PE.matmul(bank[bk][:, 0:CW], wrT[a][:, k, :], xnT[c][x][:, k, :],
                                   start=(k == 0 and n == 0), stop=(k == KD - 1 and n == 2))
            m = pe.mark(mm)
            wait(ACTE, m, small_free.get("logitsT"))
            bank_free[bk] = m = act.mark(ACTE.activation(logitsT[:], bank[bk][0:E, 0:CW], ACT.Copy))
            yield
            bk = next_bank()
            wait(PE, m, bank_free[bk])
            for j in range(CT):
                tr = PE.transpose(bank[bk][0:N, E * j:E * j + E], logitsT[:, N * j:N * j + N],
                                  ident32[0:E, 0:E])
            m = small_free["logitsT"] = pe.mark(tr)
            yield
            wait(DVE, m, small_free.get("rank"))
            bank_free[bk] = m = dve.mark(DVE.tensor_copy(
                logits[:], bank[bk][0:N, 0:CT * E].rearrange("n (j e) -> n j e", j=CT)))
            wait(DVE, m)
            for j in range(CT):
                m = dve.mark(DVE.max(top[:, j, :], logits[:, j, :]))
            wait(ACTE, m)
            tanh = act.mark(ACTE.activation(gate[:], top[:, :, 0], ACT.Tanh, scale=0.5))
            yield
            wait(DVE, m)
            for j in range(CT):
                m = dve.mark(DVE.max_index(top_index[:, j, :], top[:, j, :], logits[:, j, :]))
            wait(DVE, tanh)
            g = dve.mark(DVE.tensor_scalar(gate[:], gate[:], 0.5, 0.5, MULT, ADD))
            wait(DVE, m)
            m = dve.mark(DVE.tensor_copy(expert[:], top_index[:, :, 0]))
            wait(DVE, g)
            g = dve.mark(DVE.tensor_tensor(gate_rstd[:], gate[:], ln_rstd[:, s], MULT))
            wait(DVE, m)
            hot = dve.mark(DVE.tensor_tensor(
                onehot[:], columns[:].unsqueeze(1).to_broadcast([N, CT, E]),
                expert[:].unsqueeze(2).to_broadcast([N, CT, E]), ALU.is_equal))
            yield
            bk = next_bank()
            wait(PE, hot, bank_free[bk])
            done = counted[:, c % 2, :]
            for j in range(CT):
                o = bank[bk][0:N, E * j:E * j + E]
                terms = [(before, onehot[:, j, :])] + [(ones16, onehot[:, i, :]) for i in range(j)]
                terms.append((ones16, done))
                for n, (a, x) in enumerate(terms):
                    mm = PE.matmul(o, a[:], x, start=(n == 0), stop=(n == len(terms) - 1))
            ranked = pe.mark(mm)
            for j in range(CT):
                i = next_rows()
                wait(DVE, g, rows_free[i])
                m = xs_done[c] = dve.mark(DVE.tensor_scalar(
                    rows[i][0:N, :], x_all[:, b0 + j, :], ln_mv[:, b0 + j, 0:1],
                    gate_rstd[:, j:j + 1], SUB, MULT))
                wait(POOL, m)
                t0 = N * (b0 + j)
                rows_free[i] = rows_out[i].mark(
                    POOL.dma_start(gated_rows[t0:t0 + N, :], rows[i][0:N, :]), 16)
                if j % 2 == 1:
                    yield
            wait(DVE, hot, small_free.get("counts"))
            m = dve.mark(DVE.tensor_reduce(chunk_count[:], onehot[:].rearrange("n j e -> n e j"), AX.X, ADD))
            wait(DVE, ranked)
            bank_free[bk] = m2 = dve.mark(DVE.tensor_tensor(
                place[:], bank[bk][0:N, 0:CT * E].rearrange("n (j e) -> n j e", j=CT),
                list_base[:].unsqueeze(1).to_broadcast([N, CT, E]), ADD))
            wait(DVE, m)
            small_free["counts"] = dve.mark(
                DVE.tensor_tensor(counted[:, (c + 1) % 2, :], chunk_count[:], done, ADD))
            wait(DVE, m2)
            m = small_free["rank"] = dve.mark(DVE.tensor_tensor(place[:], place[:], onehot[:], MULT))
            yield
            wait(DVE, m)
            m = dve.mark(DVE.tensor_reduce(slot_f[:], place[:], AX.X, ADD))
            wait(DVE, m)
            m = dve.mark(DVE.tensor_copy(slot[:, s], slot_f[:]))
            wait(POOL, m, lists_cleared)
            for b in range(b0, b0 + CT):
                small_free["table"] = table_io.mark(POOL.indirect_dma_start(
                    lists, bass.IndirectOffsetOnAxis(ap=slot[:, b:b + 1], axis=0),
                    token_id[:, b:b + 1], None), 16)
            wait(PE, small_free["counts"])
            yield

        yield from route(0)
        for _ in range(len(raw)):
            shared_w.split(1, reload=False)
            yield
        yield "attention over"

        ring = (0, 1, 2, 3)
        NUNIT = 3
        raw += [buf(f"w_raw{i}", [P, PART], F32) for i in range(len(raw), NRAW)]
        xnT += [[buf(f"xnT_{p}{c}", [P, KD, CW], F32R) for p in ("hi", "lo")] for c in range(len(xnT), NCH)]
        w_split += [[[buf(f"w{n}{s}_{p}", [P, PART], F32R) for p in ("hi", "lo")] for n in ("gate", "up", "down")]
                    for s in range(1, NUNIT)]
        hT = [[buf("hT_hi0", [P, KF, CW], F32R), buf("hT_lo0", [P, KF, CW], F32R)],
              [buf("hT_hi1", [P, KF, CW], F32R), carve_f32r(P, [KF, CW], F32R)]]
        hidden = [carve(P, [CW], F32), buf("hidden1", [P, CW], F32)]
        y_rows = [buf(f"y_rows{i}", [P, D], F32) for i in range(NT)]

        def gate_up_product(n, wu, xs, width, w_ready, x_ready):
            hi, lo = (t[:, :, 0:width] for t in hT[n % 2])
            for j in range(KF):
                banks = []
                for which in range(2):
                    bk = next_bank()
                    banks.append(bk)
                    wait(PE, w_ready[which], x_ready, bank_free[bk])
                    w = [t[:].rearrange("p (k f) -> p k f", k=KD) for t in wu[which]]
                    for k in range(KD):
                        for i, (a, x) in enumerate(((0, 0), (0, 1), (1, 0))):
                            mm = PE.matmul(bank[bk][:, 0:width], w[a][:, k, P * j:P * j + P], xs[x][:, k, :],
                                           start=(k == 0 and i == 0), stop=(k == KD - 1 and i == 2))
                    m = pe.mark(mm)
                    between()
                    h = hidden[j % 2][:, 0:width]
                    if which == 0:
                        wait(ACTE, m, hidden_free[j % 2])
                        m = bank_free[bk] = act.mark(ACTE.activation(h, bank[bk][:, 0:width], ACT.Silu))
                        wait(DVE, m)
                    else:
                        wait(DVE, m)
                        m = bank_free[bk] = dve.mark(DVE.tensor_tensor(h, bank[bk][:, 0:width], h, MULT))
                wait(ACTE, m, hT_free[n % 2])
                high = act.mark(ACTE.activation(hi[:, j, :], h, ACT.Copy))
                wait(DVE, high)
                hidden_free[j % 2] = low = dve.mark(DVE.tensor_tensor(
                    lo[:, j, :], h, hi[:, j, :].bitcast(F32), SUB))
            return low

        hidden_free = [None] * 2
        hT_free = [None] * 2

        def down_product(n, wd, r0, n_r, bk, w_ready, h_ready, first, last):
            hi, lo = hT[n % 2]
            wait(PE, w_ready, h_ready, bank_free[bk])
            w = [t[:].rearrange("p (k n) -> p k n", k=KF) for t in wd]
            for j in range(KF):
                for i, (h, a) in enumerate(((hi, 0), (hi, 1), (lo, 0))):
                    mm = PE.matmul(bank[bk][0:n_r, :], h[:, j, r0:r0 + n_r], w[a][:, j, :],
                                   start=(first and j == 0 and i == 0),
                                   stop=(last and j == KF - 1 and i == 2))
            return pe.mark(mm)

        shared_w.load(NRAW)
        shared_w.split(4)
        routes = (step for c in range(1, NCH) for step in route(c))

        def between():
            next(routes, None)
            next(routes, None)

        x2_done = [None] * B

        def shared_down(n, q, c, h_ready):
            for j in range(CT):
                b = CT * c + j
                bk = 4 + (CT * n + j) % 4
                m = down_product(n, w_split[q % NUNIT][2], N * j, N, bk, shared_w.ready[3 * q + 2],
                                 h_ready, True, True)
                between()
                wait(DVE, m, xs_done[c], x2_done[b])
                x2_done[b] = bank_free[bk] = dve.mark(DVE.scalar_tensor_tensor(
                    out=x_all[:, b, :], in0=bank[bk][0:N, :], scalar=gates[0:N, 1:2],
                    in1=x_all[:, b, :], op0=MULT, op1=ADD))
            hT_free[n % 2] = m
            if c == NCH - 1:
                shared_w.unit_free[q % NUNIT] = m

        pending = None
        for n, (q, c) in enumerate((q, c) for q in range(NQ) for c in range(NCH)):
            h_ready = gate_up_product(n, w_split[q % NUNIT], [t[:] for t in xnT[c]], CW,
                                      [shared_w.ready[3 * q], shared_w.ready[3 * q + 1]], xnT_ready[c])
            if pending:
                shared_down(*pending)
            pending = (n, q, c, h_ready)
            if c > 0:
                shared_w.split(1)
        shared_down(*pending)

        bk = next_bank()
        wait(PE, small_free["counts"], bank_free[bk])
        m = pe.mark(PE.matmul(bank[bk][0:N, 0:E], ones16[:], counted[:, NCH % 2, :], start=True, stop=True))
        wait(DVE, m)
        m = dve.mark(DVE.tensor_reduce(sweeps_f[:, 0:1], bank[bk][0:1, 0:E], AX.X, ALU.max))
        wait(DVE, m)
        m = dve.mark(DVE.tensor_scalar(sweep_edges[:], sweep_edges[:], sweeps_f[:, 0:1], None, ALU.is_lt))
        wait(DVE, m)
        m = dve.mark(DVE.tensor_reduce(sweeps_f[:, 1:2], sweep_edges[:], AX.X, ADD))
        wait(DVE, m)
        sweeps_ready = dve.mark(DVE.tensor_copy(sweeps[:], sweeps_f[:, 1:2]))

        for e in (PE, ACTE, DVE, POOL, SP):
            wait(e, sweeps_ready)
        wait(POOL, small_free["table"], *rows_free, *x2_done)
        wait(SP, small_free["table"])
        n_sweeps = nc.values_load(sweeps[0:1, 0:1], min_val=1, max_val=MAX_SWEEPS)
        loop_sems = ([counter(f"sweep_{n}") for n in "pe act dve ids y_rows0 y_rows1".split()]
                     + [counter(f"sweep_rows{i}") for i in range(4)]
                     + [counter(f"sweep_raw{i}") for i in range(NRAW)])
        nc.all_engine_barrier()
        with nc.Fori(0, n_sweeps) as sweep:
            wait = Waits()
            pe, act, dve, ids_io, *y_out = loop_sems[:6]
            rows_in, raw_in = loop_sems[6:10], loop_sems[10:]
            bank_free = [None] * 8
            hidden_free, hT_free = [None] * 2, [None] * 2
            y_free = [None] * NT
            stream = WeightStream([p for e in range(E) for q in range(NQ)
                                   for p in unit_parts(w_gate_up[e], w_down[e], q)],
                                  raw_in, wait, act, dve)
            by_sweep = lists.rearrange("(e s p i) o -> p e s (i o)", e=E, s=MAX_SWEEPS, i=NT)
            ids_ready = ids_io.mark(ACTE.dma_start(
                list_ids[:], by_sweep[:, :, bass.ds(sweep, 1), :].rearrange("p e s i -> p (e s) i")), 16)
            gathered, xsT_free, x_ready = {}, [None] * 2, {}
            rows_free = [None] * 4

            def gather(e):
                wait(POOL, ids_ready)
                for i in range(NT):
                    r = (NT * e + i) % 4
                    wait(POOL, rows_free[r])
                    gathered[e, i] = rows_in[r].mark(POOL.indirect_dma_start(
                        rows[r][:], None, gated_rows,
                        bass.IndirectOffsetOnAxis(ap=list_ids[:, e, i:i + 1], axis=0),
                        bounds_check=T - 1, oob_is_err=False), 16)

            def transpose_expert(e):
                for i in range(NT):
                    r = (NT * e + i) % 4
                    x_ready[e], rows_free[r] = transpose_rows(
                        rows[r][:], P, [t[:, :, P * i:P * i + P] for t in xnT[e % 2]], gathered[e, i],
                        xsT_free[e % 2])

            def expert_down(n, e, q, h_ready):
                for i in range(NT):
                    bk = 4 + NT * (e % 2) + i
                    m = down_product(n, w_split[n % NUNIT][2], P * i, P, bk, stream.ready[3 * n + 2],
                                     h_ready, q == 0, q == NQ - 1)
                    if q == NQ - 1:
                        wait(ACTE, m, y_free[i])
                        bank_free[bk] = copied = act.mark(ACTE.activation(y_rows[i][:], bank[bk][:], ACT.Copy))
                        wait(POOL, copied)
                        y_free[i] = y_out[i].mark(POOL.indirect_dma_start(
                            routed_rows, bass.IndirectOffsetOnAxis(ap=list_ids[:, e, i:i + 1], axis=0),
                            y_rows[i][:], None, bounds_check=T - 1, oob_is_err=False), 16)
                hT_free[n % 2] = stream.unit_free[n % NUNIT] = m

            gather(0)
            stream.split(3)
            transpose_expert(0)
            stream.split(3)
            pending = None
            for n, (e, q) in enumerate((e, q) for e in range(E) for q in range(NQ)):
                if q == 0 and e + 1 < E:
                    gather(e + 1)
                if q == NQ - 1 and e + 1 < E:
                    transpose_expert(e + 1)
                h_ready = gate_up_product(
                    n, w_split[n % NUNIT], [t[:, :, 0:SLOTS] for t in xnT[e % 2]], SLOTS,
                    [stream.ready[3 * n], stream.ready[3 * n + 1]], x_ready[e])
                if q == NQ - 1:
                    xsT_free[e % 2] = (pe, pe.value)
                if pending:
                    expert_down(*pending)
                pending = (n, e, q, h_ready)
                stream.split(3)
            expert_down(*pending)
            wait(POOL, *y_free, *[gathered[E - 2 + i // NT, i % NT] for i in range(2 * NT)])
            wait(SP, *y_free)
            nc.all_engine_barrier()
            POOL.dma_reset()
            for c in loop_sems:
                POOL.sem_clear(c.sem)
            nc.all_engine_barrier()

        wait = Waits()
        done = counter("final_done")
        final_in = [counter(f"final_in{i}") for i in range(NRAW)]
        stores = counter("stores")
        PB = 2
        free = [None] * NRAW
        routed_b = routed_rows.rearrange("(b n) d -> n b d", n=N)
        out_b = out.rearrange("b n d -> n b d")
        for n in range(B // PB):
            i, s = n % NRAW, slice(PB * n, PB * n + PB)
            dst = raw[i][0:N, :].rearrange("n (b d) -> n b d", b=PB)
            wait(SP, free[i])
            loaded = final_in[i].mark(SP.dma_start(dst, routed_b[:, s, :]), 16)
            wait(DVE, loaded)
            free[i] = m = done.mark(DVE.scalar_tensor_tensor(
                out=x_all[:, s, :], in0=dst, scalar=gates[0:N, 1:2], in1=x_all[:, s, :],
                op0=MULT, op1=ADD))
            wait(ACTE, m)
            stored = stores.mark(ACTE.dma_start(out_b[:, s, :], x_all[:, s, :]), 16)
        wait(ACTE, stored)


_INS = ["x", "ctx_2048", "g_xattn", "g_ffn", "L0_xattn_Wq", "L0_xattn_Wk", "L0_xattn_Wv",
        "L0_ffn_router_w", "L0_ffn_w_gate_up", "L0_ffn_w_down", "L0_ffn_shared_gate_up",
        "L0_ffn_shared_down"]


def kernel(**inputs):
    import numpy as np
    import concourse.bacc as bacc
    from concourse.bass_utils import run_bass_kernel_spmd

    nc = bacc.Bacc("TRN2", target_bir_lowering=False, num_devices=1)
    arrays, args = {}, []
    for name in _INS:
        arrays[name] = np.ascontiguousarray(inputs[name])
        args.append(nc.dram_tensor(name, arrays[name].shape, mybir.dt.from_np(arrays[name].dtype),
                                   kind="ExternalInput").ap())
    out = nc.dram_tensor("out", arrays["x"].shape, F32, kind="ExternalOutput").ap()
    build_program(nc, *args, out)
    result = run_bass_kernel_spmd(nc, [arrays], core_ids=[0])
    return result.results[0]["out"]
```

```python
from contextlib import ExitStack

import concourse.bass as bass
from concourse import mybir

F32 = mybir.dt.float32
F32R = mybir.dt.float32r
F16 = mybir.dt.float16
I32 = mybir.dt.int32
U32 = mybir.dt.uint32
ALU = mybir.AluOpType
ACT = mybir.ActivationFunctionType
AX = mybir.AxisListType

P = 128
LN_EPS = 1e-5
RMS_EPS = 1e-6
RSQRT_MAGIC = 0x5F3759DF


class Counter:

    def __init__(self, sem):
        self.sem, self.value = sem, 0

    def mark(self, instruction, by=1):
        instruction.then_inc(self.sem, by)
        self.value += by
        return self, self.value


class Waits:

    def __init__(self):
        self.seen = {}

    def __call__(self, engine, *marks):
        for mark in marks:
            if mark is None:
                continue
            counter, value = mark
            key = (engine.engine, counter.sem.name)
            if self.seen.get(key, 0) < value:
                engine.wait_ge(counter.sem, value)
                self.seen[key] = value


class Core:
    pass


def rsqrt_step(v, wait, done, y, t, x, ready, i):
    wait(v, ready)
    if i == 0:
        return done.mark(v.tensor_scalar(y.bitcast(I32), x.bitcast(I32), -0.5, float(RSQRT_MAGIC),
                                         ALU.mult, ALU.add))
    if i % 4 == 1:
        return done.mark(v.tensor_tensor(t, y, y, ALU.mult))
    if i % 4 == 2:
        return done.mark(v.tensor_tensor(t, t, x, ALU.mult))
    if i % 4 == 3:
        return done.mark(v.tensor_scalar(t, t, -0.5, 1.5, ALU.mult, ALU.add))
    return done.mark(v.tensor_tensor(y, y, t, ALU.mult))


RSQRT_STEPS = 13

T_SLOTS = (-3, 0, 9, 17)
RMS_SLOTS = (1, 1) + 12 * (2,)
PACK_SLOTS = (8, 10, 12, 15)
PACK_T_SLOTS = ((11, 12), (13, 14), (15, 16), (18, 20))
PV_LAG = 3
X1_SLOT = 13


def build_program(nc, x, ctx, g_xattn, g_ffn, w_q, w_k, w_v, w_router, w_gate_up, w_down,
                  w_sh_gate_up, w_sh_down, out):
    B, N, D = x.shape
    KD = D // P
    NMT = -(-ctx.shape[1] // P)

    stack = ExitStack()
    with stack:
        def sb(name, shape, dt, scope=stack):
            return scope.enter_context(nc.sbuf_tensor(name, shape, dt))

        def counter(name):
            return Counter(stack.enter_context(nc.semaphore(name)))

        bank = [stack.enter_context(nc.psum_tensor(f"bank{i}", [P, 512], F32)) for i in range(8)]
        wait = Waits()
        pe, act, dve, pool = (counter(n) for n in ("pe_done", "act_done", "dve_done", "pool_done"))
        ACTE, DVE, POOL, SP = nc.scalar, nc.vector, nc.gpsimd, nc.sync

        ident32 = sb("ident32", [P, P], F32)
        ident16 = sb("ident16", [P, P], F16)
        gates = sb("gates", [P, 2], F32)
        x_all = sb("x_all", [N, B, D], F32)
        ln_stats = sb("ln_stats", [N, B, 6], F32)
        ln_mv = sb("ln_mv", [N, B, 2], F32)
        ln_var = sb("ln_var", [N, B], F32)
        ln_rstd = sb("ln_rstd", [N, B], F32)
        ln_tmp = sb("ln_tmp", [N, B], F32)

        m = pool.mark(POOL.memset(ident32[:], 0.0))
        wait(POOL, m)
        identity_ready = pool.mark(POOL.affine_select(
            out=ident32[:], in_=ident32[:], compare_op=ALU.not_equal, fill=1.0, base=0,
            pattern=[[-1, P]], channel_multiplier=1))
        wait(DVE, identity_ready)
        identity16_ready = dve.mark(DVE.tensor_copy(ident16[:], ident32[:]))

        x_in = [counter(f"x_in{i}") for i in range(4)]
        XC = B // len(x_in)

        def load_x(i):
            return x_in[i].mark(SP.dma_start(
                x_all[:, XC * i:XC * i + XC, :], x[XC * i:XC * i + XC].rearrange("b n d -> n b d")), 16)

        g_in = counter("g_in")
        for i, g in enumerate((g_xattn, g_ffn)):
            gates_loaded = g_in.mark(ACTE.dma_start(
                gates[:, i:i + 1], g.rearrange("(a n) -> a n", a=1).to_broadcast([P, 1])), 16)

        bank_free = [None] * 8
        x1_done = [None] * B
        arena_f32r = sb("arena_f32r", [P, 2 * 3 * KD * D + 2 * 2 * KD * P + 32], F32R)
        arena_f32 = sb("arena_f32", [P, (5 + 1 + 1 + NMT + 1) * D], F32)
        rstd_ready = [None] * (B // XC)
        core = Core()
        core.nc, core.sb, core.counter, core.wait = nc, sb, counter, wait
        core.bank, core.bank_free = bank, bank_free
        core.pe, core.act, core.dve, core.pool = pe, act, dve, pool
        core.ident32, core.ident16 = ident32, ident16
        core.identity_ready, core.identity16_ready = identity_ready, identity16_ready
        core.x_all, core.XC, core.load_x = x_all, XC, load_x
        core.gates, core.gates_loaded = gates, gates_loaded
        core.ln_stats, core.ln_mv, core.ln_var, core.ln_rstd, core.ln_tmp = (
            ln_stats, ln_mv, ln_var, ln_rstd, ln_tmp)
        core.rstd_ready, core.x1_done = rstd_ready, x1_done
        core.arena_f32r, core.arena_f32 = arena_f32r, arena_f32
        core.moe = feed_forward(core, w_router, w_gate_up, w_down, w_sh_gate_up, w_sh_down, out)
        core.moe_at = None
        attention(core, ctx, w_q, w_k, w_v)
        while core.moe_at != "attention over":
            core.moe_at = next(core.moe)
        for e in (ACTE, DVE, POOL, SP):
            wait(e, x1_done[B - 1])
        for _ in core.moe:
            pass


def carver(arena):
    offset = 0

    def carve(rows, shape, dt):
        nonlocal offset
        count = 1
        for n in shape:
            count *= n
        words = -(-count * mybir.dt.size(dt) // 4)
        view = arena[0:rows, offset:offset + words]
        offset += words
        assert offset <= arena.shape[1]
        if dt != arena.dtype:
            view = view.bitcast(dt)[:, 0:count]
        if len(shape) == 1:
            return view
        names = " ".join("abcd"[:len(shape)])
        return view.rearrange(f"p ({names}) -> p {names}", **dict(zip("abcd", shape)))

    return carve


def attention(core, ctx, w_q, w_k, w_v):
    nc, sb, counter, wait = core.nc, core.sb, core.counter, core.wait
    PE, ACTE, DVE, POOL, SP = nc.tensor, nc.scalar, nc.vector, nc.gpsimd, nc.sync
    pe, act, dve, pool = core.pe, core.act, core.dve, core.pool
    bank, bank_free = core.bank, core.bank_free
    ident32, ident16, x_all, gates, XC = core.ident32, core.ident16, core.x_all, core.gates, core.XC
    ln_stats, ln_mv, ln_var, ln_rstd, ln_tmp = (
        core.ln_stats, core.ln_mv, core.ln_var, core.ln_rstd, core.ln_tmp)
    rstd_ready, x1_done = core.rstd_ready, core.x1_done
    N, B, D = x_all.shape
    M = ctx.shape[1]
    HD = 16
    H = D // HD
    KD = D // P
    HPAIR = H // 2
    HROW = P // 2
    GH = 4
    NG = H // GH
    MT = [(r, min(P, M - r)) for r in range(0, M, P)]
    NMT = len(MT)
    VW = 2 * HD + 1
    SCALE = float(HD) ** -0.5
    MULT, ADD, SUB = ALU.mult, ALU.add, ALU.subtract
    scope = ExitStack()
    with scope:
        def buf(name, shape, dt):
            return sb(name, shape, dt, scope)

        carve_f32r, carve = carver(core.arena_f32r), carver(core.arena_f32)
        wqT = [carve_f32r(P, [KD, D], F32R) for _ in range(2)]
        wkvT = [carve_f32r(P, [KD, 2, D], F32R) for _ in range(2)]
        NRAW = 5
        raw = [carve(P, [D], F32) for i in range(NRAW)]
        raw_in = [counter(f"raw_in{i}") for i in range(NRAW)]
        raw_free = [None] * NRAW
        srcT = [[carve_f32r(P, [KD, P], F32R) for _ in range(2)] for i in range(2)]
        xn = carve(N, [D], F32)
        square = carve(P, [D], F32)
        k_raw = carve(P, [NMT, D], F32)
        q_raw = carve(N, [D], F32)
        sumsq = [buf(f"sumsq{i}", [P, NMT + 1, H], F32) for i in range(2)]
        rms = [buf(f"rms{i}", [P, NMT + 1, H], F32) for i in range(2)]
        rms_tmp = buf("rms_tmp", [P, NMT + 1, H], F32)
        normed = [buf(f"normed{i}", [P, D], F32) for i in range(2)]
        k_pack = [buf(f"k_pack{t}", [P, H, HROW], F16) for t in range(NMT)]
        q_pack = buf("q_pack", [N, H, HROW], F16)
        kT = [buf(f"kT{i}", [P, HPAIR, NMT * P], F16) for i in range(2)]
        qT = [buf(f"qT{i}", [P, HPAIR, 2 * N], F16) for i in range(2)]
        v_pack = [buf(f"v_pack{i}", [P, NMT, H, VW], F16) for i in range(3)]
        NPR = 2
        probs = [buf(f"probs{i}", [P, 2, GH, N], F32) for i in range(NPR)]
        probs_hi = [buf(f"probs_hi{i}", [P, 2, GH, P], F16) for i in range(NPR)]
        probs_lo = [buf(f"probs_lo{i}", [P, 2, GH, P], F16) for i in range(NPR)]
        heads_out = buf("heads_out", [N, H, VW], F32)
        inv_sum = buf("inv_sum", [N, H], F32)

        for t in v_pack:
            m = pool.mark(POOL.memset(t[:, :, :, HD:HD + 1], 1.0))
        for t in sumsq:
            m = pool.mark(POOL.memset(t[:], 1.0))
        for t in k_pack + [q_pack] + qT + probs_hi + probs_lo:
            m = pool.mark(POOL.memset(t[:].bitcast(F32), 0.0))
        constants_ready = m

        n_raw = 0

        def load_rows(src):
            nonlocal n_raw
            i = n_raw % NRAW
            n_raw += 1
            wait(SP, raw_free[i])
            ready = raw_in[i].mark(SP.dma_start(raw[i][0:src.shape[0], :], src), 16)
            return i, ready

        ctx_tiles = [(b, t) for b in range(B) for t in range(NMT)]
        ctx_loaded = {}

        def prefetch_ctx():
            if len(ctx_loaded) < len(ctx_tiles):
                b, t = ctx_tiles[len(ctx_loaded)]
                r, m = MT[t]
                ctx_loaded[b, t] = load_rows(ctx[b, r:r + m, :])

        weights = [(w, j) for w in (w_k, w_v, w_q) for j in range(KD)]
        early = 2 * KD
        w_loaded, w_turned = [], [None] * len(weights)
        w_bank = [(0, 2, 3, 4, 5, 6)[n % 6] for n in range(early)] + [4, 5, 6, 7]

        def load_weight():
            if len(w_loaded) < len(weights):
                w, j = weights[len(w_loaded)]
                w_loaded.append(load_rows(w[P * j:P * j + P, :]))
            else:
                prefetch_ctx()

        def weight_views(n):
            w, j = weights[n]
            if w is w_q:
                src = bank[w_bank[n]][:].rearrange("p (k c) -> p k c", k=KD)
                return src, *(t[:, :, P * j:P * j + P] for t in wqT)
            src = bank[w_bank[n]][:].rearrange("p (k c s) -> p k s c", k=KD, s=2)
            c0 = (D // 2 if w is w_v else 0) + P // 2 * j
            return src, *(t[:, :, :, c0:c0 + P // 2] for t in wkvT)

        def weight_on_pe(n):
            i, ready = w_loaded[n]
            bk = w_bank[n]
            wait(PE, ready, bank_free[bk])
            for k in range(KD):
                tr = PE.transpose(bank[bk][:, P * k:P * k + P], raw[i][:, P * k:P * k + P], ident32[:])
            raw_free[i] = w_turned[n] = pe.mark(tr)
            load_weight()

        def weight_on_act(n):
            src, hi, lo = weight_views(n)
            wait(ACTE, w_turned[n])
            w_turned[n] = act.mark(ACTE.activation(hi, src, ACT.Copy))

        def weight_on_dve(n):
            src, hi, lo = weight_views(n)
            wait(DVE, w_turned[n])
            w_turned[n] = bank_free[w_bank[n]] = dve.mark(
                DVE.tensor_tensor(lo, src, hi.bitcast(F32), SUB))

        for _ in range(NRAW):
            load_weight()
        wait(PE, core.identity_ready)
        for n in range(early):
            weight_on_pe(n)
            weight_on_act(n)
            weight_on_dve(n)

        units = [(g, t) for g in range(NG) for t in range(NMT)]
        WINDOW = len(units)
        agenda = {}

        def at(slot, engine, step, *args):
            agenda.setdefault((slot, engine), []).append((step, args))

        mark = {}
        prj_ring, tr_ring = [0], [0]

        def next_prj_bank():
            prj_ring[0] += 1
            return (2, 3)[prj_ring[0] % 2]

        def next_tr_bank():
            tr_ring[0] += 1
            return (0, 1)[tr_ring[0] % 2]

        def transpose_source(slot, b, t):
            side = t % 2
            rows = MT[t][1] if t < NMT else N

            def on_pe():
                if t < NMT:
                    i, ready = ctx_loaded[b, t]
                    src = raw[i][0:rows, :]
                else:
                    src, ready = xn[:], mark["xn", b]
                bk = mark["bank", b, t] = next_tr_bank()
                wait(PE, ready, bank_free[bk])
                for k in range(KD):
                    tr = PE.transpose(bank[bk][:, P * k:P * k + rows], src[:, P * k:P * k + P],
                                      ident32[0:rows, 0:rows])
                mark["T", b, t] = transposed = pe.mark(tr)
                if t < NMT:
                    raw_free[i] = transposed
                    prefetch_ctx()
                else:
                    mark["xn free"] = transposed

            def views():
                psum = bank[mark["bank", b, t]][:].rearrange("p (k r) -> p k r", k=KD)[:, :, 0:rows]
                return psum, *(s[:, :, 0:rows] for s in srcT[side])

            def on_act():
                psum, hi, lo = views()
                wait(ACTE, mark["T", b, t], mark.get(("src free", side)))
                mark["src high", b, t] = act.mark(ACTE.activation(hi, psum, ACT.Copy))

            def on_dve():
                psum, hi, lo = views()
                wait(DVE, mark["src high", b, t])
                mark["src", b, t] = bank_free[mark["bank", b, t]] = dve.mark(
                    DVE.tensor_tensor(lo, psum, hi.bitcast(F32), SUB))

            at(slot, "pe", on_pe)
            at(slot + 1, "act", on_act)
            at(slot + 2, "dve", on_dve)

        def project(slots, b, t, weight):
            side = t % 2
            rows = MT[t][1] if t < NMT else N
            name = "prj", b, t, weight
            w = {"q": wqT, "k": [a[:, :, 0, :] for a in wkvT], "v": [a[:, :, 1, :] for a in wkvT]}[weight]
            products = [(k, a, c) for k in range(KD) for a, c in ((0, 0), (0, 1), (1, 0))]

            def on_pe(n):
                k, a, c = products[n]
                if n == 0:
                    mark["bank", name] = bk = next_prj_bank()
                    wait(PE, mark["src", b, t], bank_free[bk])
                mm = PE.matmul(bank[mark["bank", name]][0:rows, :], srcT[side][a][:, k, 0:rows],
                               w[c][:, k], start=(n == 0), stop=(n == len(products) - 1))
                if n == len(products) - 1:
                    mark[name] = mark["src free", side] = pe.mark(mm)

            for n, slot in enumerate(slots):
                at(slot, "pe", on_pe, n)

        def take_heads(slot, b, t, weight):
            rows, dst = (MT[t][1], k_raw[0:MT[t][1], t, :]) if t < NMT else (N, q_raw[:])
            name = "prj", b, t, weight

            def copy():
                wait(ACTE, mark[name], mark.get(("scaled", b - 1, t)))
                mark["raw", b, t] = act.mark(ACTE.activation(
                    dst, bank[mark["bank", name]][0:rows, :], ACT.Copy))

            def take_square():
                wait(ACTE, mark.get("square free"))
                mark["square"] = bank_free[mark["bank", name]] = act.mark(ACTE.activation(
                    square[0:rows, :], bank[mark["bank", name]][0:rows, :], ACT.Square))

            def reduce():
                wait(DVE, mark["square"], mark.get(("rms", b - 2)))
                mark["sumsq", b, t] = mark["square free"] = dve.mark(DVE.tensor_reduce(
                    sumsq[b % 2][0:rows, t, :],
                    square[0:rows, :].rearrange("p (h d) -> p h d", d=HD), AX.X, ADD))

            at(slot, "act", copy)
            at(slot, "act", take_square)
            at(slot + 1, "dve", reduce)

        def take_values(slot, b, t):
            name = "prj", b, t, "v"
            m = MT[t][1]
            vp = v_pack[b % 3][0:m, t]

            def psum():
                return bank[mark["bank", name]][0:m, :].rearrange("p (h d) -> p h d", d=HD)

            def on_act():
                wait(ACTE, mark[name], mark.get(("values", b - 3)))
                mark["v high", b, t] = act.mark(ACTE.activation(vp[:, :, 0:HD], psum(), ACT.Copy))

            def on_dve():
                wait(DVE, mark["v high", b, t])
                mark["v", b] = bank_free[mark["bank", name]] = dve.mark(
                    DVE.tensor_tensor(vp[:, :, HD + 1:VW], psum(), vp[:, :, 0:HD], SUB))

            at(slot, "act", on_act)
            at(slot + 1, "dve", on_dve)

        def normalise_x(slot, b):
            def on_dve():
                wait(DVE, mark["stats", b // XC], mark.get("xn free"))
                mark["xn", b] = dve.mark(DVE.tensor_scalar(
                    xn[:], x_all[:, b, :], ln_mv[:, b, 0:1], ln_rstd[:, b:b + 1], SUB, MULT))
            at(slot, "dve", on_dve)

        def rms_factors(slots, b):
            s = sumsq[b % 2][:]

            def mean():
                wait(DVE, *[mark["sumsq", b, t] for t in range(NMT + 1)],
                     mark.get(("scaled", b - 2, NMT)))
                mark["rms", b] = dve.mark(DVE.tensor_scalar(s, s, 1.0 / HD, RMS_EPS, MULT, ADD))

            on_vector = b == 0

            def step(i):
                engine, done = (DVE, dve) if i == 0 or on_vector else (POOL, pool)
                mark["rms", b] = rsqrt_step(engine, wait, done, rms[b % 2][:], rms_tmp[:], s,
                                            mark["rms", b], i)

            at(slots[0], "dve", mean)
            for i, slot in enumerate(slots[1:]):
                at(slot, "dve" if i == 0 or on_vector else "pool", step, i)

        def make_pack(slot, b, t):
            if t < NMT:
                rows, src, pack, places, low_place = MT[t][1], k_raw[:, t, :], k_pack[t], (0, 2 * HD), HD
            else:
                rows, src, pack, places, low_place = N, q_raw[:], q_pack, (0, HD), 2 * HD
            n = normed[t % 2][0:rows, :]
            nh = n.rearrange("p (h d) -> p h d", d=HD)

            def scale():
                wait(DVE, mark["rms", b], mark["raw", b, t], mark.get(("normed free", t % 2)))
                mark["scaled", b, t] = dve.mark(DVE.tensor_tensor(
                    nh, src[0:rows].rearrange("p (h d) -> p h d", d=HD),
                    rms[b % 2][0:rows, t, :].unsqueeze(2).to_broadcast([rows, H, HD]), MULT))

            def high():
                a, c = places
                wide = pack[0:rows, :, a:c + HD].rearrange(
                    "p h (s d) -> p h s d", d=HD)[:, :, ::(c - a) // HD, :]
                wait(ACTE, mark["scaled", b, t], mark.get(("pack transposed", b - 1, t)))
                mark["pack high", b, t] = act.mark(ACTE.activation(
                    wide, nh.unsqueeze(2).to_broadcast([rows, H, 2, HD]), ACT.Copy))

            engine, done, name = (DVE, dve, "dve") if b == 0 else (POOL, pool, "pool")

            def low():
                wait(engine, mark["pack high", b, t])
                mark["pack", b, t] = mark["normed free", t % 2] = done.mark(engine.tensor_tensor(
                    pack[0:rows, :, low_place:low_place + HD], nh,
                    pack[0:rows, :, places[0]:places[0] + HD], SUB))

            at(slot, "dve", scale)
            at(slot + 1, "act", high)
            at(slot + 2, name, low)

        def transpose_pack(slot, b, t, half):
            pack, rows = (k_pack[t], P) if t < NMT else (q_pack, N)
            name = "bank", "pack", b, t, half
            pairs = slice(HPAIR // 2 * half, HPAIR // 2 * (half + 1))

            def psum():
                return bank[mark[name]][:].bitcast(F16).rearrange("p (a r) -> p a r", a=HPAIR // 2)

            def on_pe():
                bk = mark[name] = next_tr_bank()
                wait(PE, mark["pack", b, t], bank_free[bk])
                for a in range(HPAIR // 2):
                    pair = HPAIR // 2 * half + a
                    tr = PE.transpose(psum()[:, a, 0:rows], pack[0:rows, 2 * pair:2 * pair + 2, :]
                                      .rearrange("p a c -> p (a c)"), ident16[0:rows, 0:rows])
                mark["pack transposed", b, t] = mark["pack T", b, t, half] = pe.mark(tr)

            def on_act():
                wait(ACTE, mark["pack T", b, t, half], mark.get(("scored", b - 2)))
                if t < NMT:
                    m = act.mark(ACTE.activation(
                        kT[b % 2][:, pairs, P * t:P * t + P].bitcast(F32), psum().bitcast(F32), ACT.Copy))
                else:
                    for z in range(2):
                        rows_z = slice(HROW * z, HROW * z + HROW)
                        m = act.mark(ACTE.activation(
                            qT[b % 2][rows_z, pairs, N * z:N * z + N].bitcast(F32),
                            psum()[rows_z, :, 0:N].bitcast(F32), ACT.Copy))
                mark["kT", b] = bank_free[mark[name]] = m

            at(slot, "pe", on_pe)
            at(slot + 1, "act", on_act)

        def unit(s):
            return (s // WINDOW, *units[s % WINDOW]) if 0 <= s < B * WINDOW else None

        sc_banks, pv_banks = (4, 5), (6, 7)

        def scores(s):
            b, g, t = unit(s)
            bk = sc_banks[s % 2]
            wait(PE, mark["kT", b], bank_free[bk])
            for a in range(GH // 2):
                pair = GH // 2 * g + a
                mm = PE.matmul(bank[bk][:, 2 * N * a:2 * N * (a + 1)],
                               kT[b % 2][:, pair, P * t:P * t + P], qT[b % 2][:, pair, :],
                               start=True, stop=True)
            mark["scored", b] = mark["scores", s % 2] = pe.mark(mm)

        def exp_scores(s):
            bk = sc_banks[s % 2]
            i = s // 2 % NPR
            wait(ACTE, mark["scores", s % 2], mark.get(("probs free", i)))
            mark["probs", i] = bank_free[bk] = act.mark(ACTE.activation(
                probs[i][:, s % 2], bank[bk][:, 0:GH * N].rearrange("p (h n) -> p h n", h=GH),
                ACT.Exp, scale=SCALE))

        def split_high(s):
            i = (s - 2) // 2 % NPR
            wait(DVE, mark["probs", i], mark.get(("split free", i)))
            mark["high", i] = dve.mark(DVE.tensor_copy(probs_hi[i][:, :, :, 0:N], probs[i][:]))

        def split_low(s):
            i = (s - 2) // 2 % NPR
            wait(DVE, mark["high", i])
            mark["split", i] = mark["probs free", i] = dve.mark(DVE.tensor_tensor(
                probs_lo[i][:, :, :, 0:N], probs[i][:], probs_hi[i][:, :, :, 0:N], SUB))

        def weighted_values(s):
            b, g, t = unit(s)
            bk = pv_banks[g % 2]
            m = MT[t][1]
            i = s // 2 % NPR
            wait(PE, mark["split", i], mark["v", b], bank_free[bk])
            for h in range(GH):
                v = v_pack[b % 3][0:m, t, GH * g + h, :]
                col = VW * h
                PE.matmul(bank[bk][:, col:col + VW], probs_hi[i][0:m, s % 2, h, :], v,
                          start=(t == 0 and h == 0), stop=False, skip_group_check=True)
                mm = PE.matmul(bank[bk][:, col:col + HD + 1], probs_lo[i][0:m, s % 2, h, :], v[:, 0:HD + 1],
                               start=False, stop=(t == NMT - 1 and h == GH - 1),
                               skip_group_check=True)
            mark["split free", i] = mark["values", b] = pe.mark(mm)

        def take_outputs(b, g, heads_free):
            bk = pv_banks[g % 2]
            wait(ACTE, mark["values", b], heads_free())
            mark["heads", b] = bank_free[bk] = act.mark(ACTE.activation(
                heads_out[:, GH * g:GH * g + GH, :],
                bank[bk][0:N, 0:GH * VW].rearrange("p (h c) -> p h c", h=GH), ACT.Copy))

        def finish_attention(slot, b):
            o = heads_out[:, :, 0:HD]
            xb = x_all[:, b, :].rearrange("p (h d) -> p h d", d=HD)

            def invert():
                wait(DVE, mark["heads", b], mark["gates"])
                mark["inv"] = dve.mark(DVE.reciprocal(inv_sum[:], heads_out[:, :, HD]))

            def add_parts():
                mark["o"] = dve.mark(DVE.tensor_tensor(o, heads_out[:, :, 0:HD],
                                                       heads_out[:, :, HD + 1:VW], ADD))

            def divide():
                wait(DVE, mark["inv"], mark["o"])
                mark["o"] = dve.mark(DVE.tensor_tensor(
                    o, o, inv_sum[:].unsqueeze(2).to_broadcast([N, H, HD]), MULT))

            def add_to_x():
                wait(DVE, mark["o"])
                x1_done[b] = mark["x1", b] = dve.mark(DVE.scalar_tensor_tensor(
                    out=xb, in0=o, scalar=gates[0:N, 0:1], in1=xb, op0=MULT, op1=ADD))

            at(slot, "dve", invert)
            at(slot, "dve", add_parts)
            at(slot + 1, "dve", divide)
            at(slot + 2, "dve", add_to_x)

        PJ = 3 * KD
        projections = [(t, w) for t in range(NMT) for w in ("v", "k")] + [(NMT, "q")]
        pj_slots = [n * WINDOW // (PJ * len(projections)) for n in range(PJ * len(projections))]
        for j in range(KD):
            at(-2 * WINDOW + T_SLOTS[0] - KD + j, "pe", weight_on_pe, early + j)
            at(-2 * WINDOW + T_SLOTS[0] - KD + j + 1, "act", weight_on_act, early + j)
            at(-2 * WINDOW + T_SLOTS[0] - KD + j + 2, "dve", weight_on_dve, early + j)

        def layer_norm(slot, c, name, ready):
            group = range(XC * c, XC * c + XC)
            ch = slice(XC * c, XC * c + XC)

            def stats(b):
                wait(DVE, ready())
                mark[name, c] = dve.mark(DVE.bn_stats(ln_stats[:, b, :], x_all[:, b, :]))

            def aggregate():
                wait(DVE, mark[name, c])
                for b in group:
                    m = dve.mark(DVE.bn_aggr(ln_mv[:, b, :], ln_stats[:, b, :]))
                wait(DVE, m)
                mark[name, c] = dve.mark(DVE.tensor_scalar(ln_var[:, ch], ln_mv[:, ch, 1], LN_EPS, None, ADD))

            def step(i):
                engine, done = (DVE, dve) if i == 0 else (POOL, pool)
                mark[name, c] = rstd_ready[c] = rsqrt_step(
                    engine, wait, done, ln_rstd[:, ch], ln_tmp[:, ch], ln_var[:, ch], mark[name, c], i)

            for j, b in enumerate(group):
                at(slot + j, "dve", stats, b)
            at(slot + XC, "dve", aggregate)
            at(slot + XC, "dve", step, 0)
            for i in range(1, RSQRT_STEPS):
                at(slot + XC, "pool", step, i)

        def request_x(i):
            mark["x", i] = core.load_x(i)

        def gate_factors():
            wait(ACTE, core.gates_loaded)
            mark["gates"] = act.mark(ACTE.activation(gates[:], gates[:], ACT.Tanh))

        at(-WINDOW, "act", gate_factors)
        for i in range(B // XC):
            at(-2 * WINDOW + 2 + 4 * i, "pe", request_x, i)
            layer_norm(-2 * WINDOW + 6 + 5 * i, i, "stats", lambda i=i: mark["x", i])
        for b in range(-2, B):
            w0 = WINDOW * b
            c, d = b + 1, b + 2
            if d < B:
                for t, slot in zip(range(NMT + 1), T_SLOTS):
                    transpose_source(w0 + slot, d, t)
                normalise_x(w0 + T_SLOTS[NMT] - 2, d)
                for i, (t, weight) in enumerate(projections):
                    slots = pj_slots[PJ * i:PJ * i + PJ]
                    project([w0 + s for s in slots], d, t, weight)
                    if weight == "v":
                        take_values(w0 + slots[-1] + 1, d, t)
                    else:
                        slot = max(slots[-1] + 1, PACK_SLOTS[0] + 1) if t == 0 else slots[-1] + 1
                        take_heads(w0 + slot, d, t, weight)
                rms_factors([w0 + WINDOW + s for s in RMS_SLOTS], d)
            if 0 <= c < B:
                for t in range(NMT + 1):
                    make_pack(w0 + PACK_SLOTS[t], c, t)
                    for half in range(2):
                        transpose_pack(w0 + PACK_T_SLOTS[t][half], c, t, half)
            if b >= 0:
                for g in range(NG):
                    at(w0 + NMT * g + NMT - 1 + PV_LAG + (2 if g < NG - 1 else 1), "act", take_outputs, b, g,
                       lambda b=b: mark.get(("x1", b - 1)))
                finish_attention(w0 + WINDOW + PV_LAG + 1, b)

        for c in range(B // XC):
            layer_norm(WINDOW * XC * (c + 1) + X1_SLOT, c, "x1 stats",
                       lambda c=c: x1_done[XC * c + XC - 1])

        def early_feed_forward():
            if core.moe_at != "attention over":
                core.moe_at = next(core.moe)

        def free_arena():
            next(core.moe)
            core.moe.send((mark["prj", B - 1, NMT, "q"], mark["square free"], mark["scaled", B - 1, NMT]))

        s0 = WINDOW * (B - 2) + PACK_SLOTS[NMT] + 1
        at(s0, "pe", free_arena)
        for slot in range(s0 + 1, WINDOW * B):
            at(slot, "pe", early_feed_forward)

        wait(PE, w_turned[early - 1], core.identity16_ready)
        wait(ACTE, constants_ready)
        wait(DVE, constants_ready)
        for s in range(min(slot for slot, _ in agenda), max(slot for slot, _ in agenda) + 1):
            if unit(s + 1):
                scores(s + 1)
            if unit(s):
                exp_scores(s)
            for step, args in agenda.get((s, "act"), []):
                step(*args)
            fills = agenda.get((s, "dve"), [])
            own = [(split_high if s % 2 == 0 else split_low, (s,))] if unit(s - 2) else []
            for i in range(max(len(fills), len(own))):
                for step, args in own[i:i + 1] + fills[i:i + 1]:
                    step(*args)
            for step, args in agenda.get((s, "pool"), []) + agenda.get((s, "pe"), []):
                step(*args)
            if unit(s - PV_LAG):
                weighted_values(s - PV_LAG)


def feed_forward(core, w_router, w_gate_up, w_down, w_sh_gate_up, w_sh_down, out):
    nc, sb, counter, wait = core.nc, core.sb, core.counter, core.wait
    PE, ACTE, DVE, POOL, SP = nc.tensor, nc.scalar, nc.vector, nc.gpsimd, nc.sync
    pe, act, dve, pool = core.pe, core.act, core.dve, core.pool
    bank, bank_free = core.bank, core.bank_free
    ident32, x_all, gates = core.ident32, core.x_all, core.gates
    ln_mv, ln_rstd, rstd_ready = core.ln_mv, core.ln_rstd, core.rstd_ready
    N, B, D = x_all.shape
    KD = D // P
    MULT, ADD, SUB = ALU.mult, ALU.add, ALU.subtract
    E, F = w_down.shape[0], w_down.shape[1]
    T = B * N
    CT = 4
    NCH = B // CT
    CW = CT * N
    FQ = 256
    NQ = F // FQ
    KF = FQ // P
    SLOTS = 2 * P
    MAX_SWEEPS = -(-T // SLOTS)
    CAP = MAX_SWEEPS * SLOTS
    NT = SLOTS // P

    gated_rows = nc.dram_tensor("gated_rows", (T, D), F32).ap()
    x2_rows = nc.dram_tensor("x2_rows", (T, D), F32).ap()
    out_rows = out.rearrange("b n d -> (b n) d")
    lists = nc.dram_tensor("expert_lists", (E * CAP, 1), I32).ap()

    scope = ExitStack()
    with scope:
        def buf(name, shape, dt):
            return sb(name, shape, dt, scope)

        carve_f32r, carve = carver(core.arena_f32r), carver(core.arena_f32)
        NRAW = 4
        PART = KD * FQ
        raw = [carve(P, [PART], F32) for i in range(2)]
        w_split = [[[carve_f32r(P, [PART], F32R) for _ in range(2)] for _ in range(3)]]
        xnT = [[carve_f32r(P, [KD, CW], F32R) for _ in range(2)] for _ in range(2)]
        wrT = [carve_f32r(P, [KD, P], F32R) for _ in range(2)]
        rows = [carve(P, [D], F32) for i in range(4)]
        logitsT = carve(E, [CW], F32)
        logits = carve(N, [CT, E], F32)
        top = carve(N, [CT, E], F32)
        top_index = carve(N, [CT, E], U32)
        expert = carve(N, [CT], F32)
        gate = carve(N, [CT], F32)
        gate_rstd = carve(N, [CT], F32)
        onehot = carve(N, [CT, E], F16)
        counted = carve(N, [2, E], F16)
        chunk_count = carve(N, [E], F32)
        place = carve(N, [CT, E], F32)
        slot_f = carve(N, [CT], F32)
        slot = carve(N, [B], I32)
        token_id = carve(N, [B], I32)
        columns = carve(N, [E], F32)
        list_base = carve(N, [E], F32)
        before = carve(N, [N], F16)
        ones16 = carve(N, [N], F16)
        sweep_edges = carve(1, [MAX_SWEEPS], F32)
        sweeps_f = carve(1, [2], F32)
        sweeps = carve(1, [1], I32)
        none_fill = carve(P, [E * CAP // P], I32)
        list_ids = carve(P, [E, NT], I32)

        arena_free = yield
        for engine in (SP, ACTE, DVE, POOL):
            wait(engine, *arena_free)

        m = pool.mark(POOL.iota(token_id[:], [[N, B]], base=0, channel_multiplier=1))
        m = pool.mark(POOL.iota(columns[:], [[1, E]], base=0, channel_multiplier=0,
                                allow_small_or_imprecise_dtypes=True))
        m = pool.mark(POOL.iota(list_base[:], [[CAP, E]], base=0, channel_multiplier=0,
                                allow_small_or_imprecise_dtypes=True))
        m = pool.mark(POOL.iota(sweep_edges[:], [[SLOTS, MAX_SWEEPS]], base=SLOTS, channel_multiplier=0,
                                allow_small_or_imprecise_dtypes=True))
        m = pool.mark(POOL.iota(none_fill[:], [[0, E * CAP // P]], base=T, channel_multiplier=0))
        filled = m
        POOL.memset(ones16[:], 1.0)
        POOL.memset(counted[:], 0.0)
        for t in rows:
            m = pool.mark(POOL.memset(t[:], 0.0))
        wait(POOL, m)
        m = pool.mark(POOL.affine_select(out=before[:], in_=ones16[:], compare_op=ALU.is_gt, fill=0.0,
                                         base=0, pattern=[[1, N]], channel_multiplier=-1))
        constants_ready = m
        lists_io = counter("lists_io")
        wait(POOL, filled)
        lists_cleared = lists_io.mark(POOL.dma_start(
            lists.rearrange("(p c) o -> p (c o)", p=P), none_fill[:]), 16)
        yield

        NUNIT = 1

        def unit_parts(gate_up, down, q):
            g = gate_up.rearrange("(k p) f -> p k f", p=P)
            d = down.rearrange("(k p) n -> p k n", p=P)
            return [g[:, :, FQ * q:FQ * q + FQ], g[:, :, F + FQ * q:F + FQ * q + FQ],
                    d[:, KF * q:KF * q + KF, :]]

        class WeightStream:

            def __init__(self, parts, raw_in, wait, act, dve):
                self.parts, self.raw_in = parts, raw_in
                self.wait, self.act, self.dve = wait, act, dve
                self.loaded, self.n_split = [], 0
                self.raw_free = [None] * NRAW
                self.unit_free = [None] * 3
                self.ready = {}
                self.load(len(raw))

            def load(self, n):
                for part in self.parts[len(self.loaded):len(self.loaded) + n]:
                    i = len(self.loaded) % NRAW
                    self.wait(SP, self.raw_free[i])
                    dst = raw[i][:].rearrange("p (a c) -> p a c", a=part.shape[1])
                    self.loaded.append(self.raw_in[i].mark(SP.dma_start(dst, part), 16))

            def split(self, n, reload=True):
                for _ in range(min(n, len(self.parts) - self.n_split)):
                    part = self.n_split
                    self.n_split += 1
                    i = part % NRAW
                    u, which = divmod(part, 3)
                    hi, lo = w_split[u % NUNIT][which]
                    self.wait(ACTE, self.loaded[part], self.unit_free[u % NUNIT])
                    high = self.act.mark(ACTE.activation(hi[:], raw[i][:], ACT.Copy))
                    self.wait(DVE, high)
                    low = self.dve.mark(DVE.tensor_tensor(lo[:], raw[i][:], hi[:].bitcast(F32), SUB))
                    self.raw_free[i] = self.ready[part] = low
                    if reload:
                        self.load(1)

        raw_in = [counter(f"w_raw_in{i}") for i in range(NRAW)]
        expert_parts = [p for e in range(E) for q in range(NQ) for p in unit_parts(w_gate_up[e], w_down[e], q)]
        stream = WeightStream([p for q in range(NQ) for p in unit_parts(w_sh_gate_up, w_sh_down, q)]
                              + expert_parts, raw_in, wait, act, dve)
        n_bank = 0
        ring = (2, 3)

        def next_bank():
            nonlocal n_bank
            n_bank += 1
            return ring[n_bank % len(ring)]

        def transpose_rows(src, n_rows, dst, ready, dst_free=None):
            bk = next_bank()
            wait(PE, ready, bank_free[bk])
            for k in range(KD):
                tr = PE.transpose(bank[bk][:, P * k:P * k + n_rows], src[:, P * k:P * k + P],
                                  ident32[0:n_rows, 0:n_rows])
            transposed = pe.mark(tr)
            psum = bank[bk][:].rearrange("p (k r) -> p k r", k=KD)[:, :, 0:n_rows]
            wait(ACTE, transposed, dst_free)
            high = act.mark(ACTE.activation(dst[0], psum, ACT.Copy))
            wait(DVE, high)
            low = dve.mark(DVE.tensor_tensor(dst[1], psum, dst[0].bitcast(F32), SUB))
            bank_free[bk] = low
            return low, transposed

        router_in = counter("router_in")
        wait(SP, constants_ready)
        router_loaded = router_in.mark(SP.dma_start(rows[0][0:E, :], w_router), 16)
        wait(DVE, constants_ready)
        for t in wrT:
            m = dve.mark(DVE.tensor_copy(t[:], rows[1][:].rearrange("p (k c) -> p k c", k=KD)))
        yield
        router_ready, transposed = transpose_rows(rows[0][0:E, :], E, [t[:, :, 0:E] for t in wrT],
                                                  router_loaded, m)
        rows_free = [transposed, None, None, None]
        n_rows = 0
        wait(PE, constants_ready)
        yield

        rows_out = [counter(f"rows_out{i}") for i in range(4)]
        table_io = counter("table_io")
        xnT_ready = [None] * NCH
        xs_done = [None] * NCH
        small_free = {}

        def next_rows():
            nonlocal n_rows
            n_rows += 1
            return (n_rows - 1) % 4

        def route(c):
            b0 = CT * c
            s = slice(b0, b0 + CT)
            r, bk = [None] * CT, [None] * CT
            normal, transposed, high = [None] * CT, [None] * CT, [None] * CT
            for step in range(CT + 3):
                j = step
                if j < CT:
                    r[j] = i = next_rows()
                    wait(DVE, rstd_ready[c], rows_free[i])
                    normal[j] = dve.mark(DVE.tensor_scalar(
                        rows[i][0:N, :], x_all[:, b0 + j, :], ln_mv[:, b0 + j, 0:1],
                        ln_rstd[:, b0 + j:b0 + j + 1], SUB, MULT))
                j = step - 3
                if 0 <= j < CT:
                    psum = bank[bk[j]][:].rearrange("p (k r) -> p k r", k=KD)[:, :, 0:N]
                    hi, lo = (t[:, :, N * j:N * j + N] for t in xnT[c])
                    wait(DVE, high[j])
                    xnT_ready[c] = bank_free[bk[j]] = dve.mark(
                        DVE.tensor_tensor(lo, psum, hi.bitcast(F32), SUB))
                j = step - 2
                if 0 <= j < CT:
                    psum = bank[bk[j]][:].rearrange("p (k r) -> p k r", k=KD)[:, :, 0:N]
                    wait(ACTE, transposed[j])
                    high[j] = act.mark(ACTE.activation(xnT[c][0][:, :, N * j:N * j + N], psum, ACT.Copy))
                j = step - 1
                if 0 <= j < CT:
                    bk[j] = next_bank()
                    wait(PE, normal[j], bank_free[bk[j]])
                    for k in range(KD):
                        tr = PE.transpose(bank[bk[j]][:, P * k:P * k + N],
                                          rows[r[j]][0:N, P * k:P * k + P], ident32[0:N, 0:N])
                    transposed[j] = rows_free[r[j]] = pe.mark(tr)
                yield
            bk = next_bank()
            wait(PE, xnT_ready[c], router_ready, bank_free[bk])
            for k in range(KD):
                for n, (a, x) in enumerate(((0, 0), (0, 1), (1, 0))):
                    mm = PE.matmul(bank[bk][:, 0:CW], wrT[a][:, k, :], xnT[c][x][:, k, :],
                                   start=(k == 0 and n == 0), stop=(k == KD - 1 and n == 2))
            m = pe.mark(mm)
            wait(ACTE, m, small_free.get("logitsT"))
            bank_free[bk] = m = act.mark(ACTE.activation(logitsT[:], bank[bk][0:E, 0:CW], ACT.Copy))
            yield
            bk = next_bank()
            wait(PE, m, bank_free[bk])
            for j in range(CT):
                tr = PE.transpose(bank[bk][0:N, E * j:E * j + E], logitsT[:, N * j:N * j + N],
                                  ident32[0:E, 0:E])
            m = small_free["logitsT"] = pe.mark(tr)
            yield
            wait(DVE, m, small_free.get("rank"))
            bank_free[bk] = m = dve.mark(DVE.tensor_copy(
                logits[:], bank[bk][0:N, 0:CT * E].rearrange("n (j e) -> n j e", j=CT)))
            wait(DVE, m)
            for j in range(CT):
                m = dve.mark(DVE.max(top[:, j, :], logits[:, j, :]))
            wait(ACTE, m)
            tanh = act.mark(ACTE.activation(gate[:], top[:, :, 0], ACT.Tanh, scale=0.5))
            yield
            wait(DVE, m)
            for j in range(CT):
                m = dve.mark(DVE.max_index(top_index[:, j, :], top[:, j, :], logits[:, j, :]))
            wait(DVE, tanh)
            g = dve.mark(DVE.tensor_scalar(gate[:], gate[:], 0.5, 0.5, MULT, ADD))
            wait(DVE, m)
            m = dve.mark(DVE.tensor_copy(expert[:], top_index[:, :, 0]))
            wait(DVE, g)
            g = dve.mark(DVE.tensor_tensor(gate_rstd[:], gate[:], ln_rstd[:, s], MULT))
            wait(DVE, m)
            hot = dve.mark(DVE.tensor_tensor(
                onehot[:], columns[:].unsqueeze(1).to_broadcast([N, CT, E]),
                expert[:].unsqueeze(2).to_broadcast([N, CT, E]), ALU.is_equal))
            yield
            bk = next_bank()
            wait(PE, hot, bank_free[bk])
            done = counted[:, c % 2, :]
            for j in range(CT):
                o = bank[bk][0:N, E * j:E * j + E]
                terms = [(before, onehot[:, j, :])] + [(ones16, onehot[:, i, :]) for i in range(j)]
                terms.append((ones16, done))
                for n, (a, x) in enumerate(terms):
                    mm = PE.matmul(o, a[:], x, start=(n == 0), stop=(n == len(terms) - 1))
            ranked = pe.mark(mm)
            for j in range(CT):
                i = next_rows()
                wait(DVE, g, rows_free[i])
                m = xs_done[c] = dve.mark(DVE.tensor_scalar(
                    rows[i][0:N, :], x_all[:, b0 + j, :], ln_mv[:, b0 + j, 0:1],
                    gate_rstd[:, j:j + 1], SUB, MULT))
                wait(POOL, m)
                t0 = N * (b0 + j)
                rows_free[i] = rows_out[i].mark(
                    POOL.dma_start(gated_rows[t0:t0 + N, :], rows[i][0:N, :]), 16)
                if j % 2 == 1:
                    yield
            wait(DVE, hot, small_free.get("counts"))
            m = dve.mark(DVE.tensor_reduce(chunk_count[:], onehot[:].rearrange("n j e -> n e j"), AX.X, ADD))
            wait(DVE, ranked)
            bank_free[bk] = m2 = dve.mark(DVE.tensor_tensor(
                place[:], bank[bk][0:N, 0:CT * E].rearrange("n (j e) -> n j e", j=CT),
                list_base[:].unsqueeze(1).to_broadcast([N, CT, E]), ADD))
            wait(DVE, m)
            small_free["counts"] = dve.mark(
                DVE.tensor_tensor(counted[:, (c + 1) % 2, :], chunk_count[:], done, ADD))
            wait(DVE, m2)
            m = small_free["rank"] = dve.mark(DVE.tensor_tensor(place[:], place[:], onehot[:], MULT))
            yield
            wait(DVE, m)
            m = dve.mark(DVE.tensor_reduce(slot_f[:], place[:], AX.X, ADD))
            wait(DVE, m)
            m = dve.mark(DVE.tensor_copy(slot[:, s], slot_f[:]))
            wait(POOL, m, lists_cleared)
            for b in range(b0, b0 + CT):
                small_free["table"] = table_io.mark(POOL.indirect_dma_start(
                    lists, bass.IndirectOffsetOnAxis(ap=slot[:, b:b + 1], axis=0),
                    token_id[:, b:b + 1], None), 16)
            wait(PE, small_free["counts"])
            yield

        yield from route(0)
        for _ in range(len(raw)):
            stream.split(1, reload=False)
            yield
        yield "attention over"

        ring = (0, 1, 2, 3)
        NUNIT = 3
        raw += [buf(f"w_raw{i}", [P, PART], F32) for i in range(len(raw), NRAW)]
        xnT += [[buf(f"xnT_{p}{c}", [P, KD, CW], F32R) for p in ("hi", "lo")] for c in range(len(xnT), NCH)]
        w_split += [[[buf(f"w{n}{s}_{p}", [P, PART], F32R) for p in ("hi", "lo")] for n in ("gate", "up", "down")]
                    for s in range(1, NUNIT)]
        hT = [[buf("hT_hi0", [P, KF, CW], F32R), buf("hT_lo0", [P, KF, CW], F32R)],
              [buf("hT_hi1", [P, KF, CW], F32R), carve_f32r(P, [KF, CW], F32R)]]
        hidden = [carve(P, [CW], F32), buf("hidden1", [P, CW], F32)]
        y_rows = [buf(f"y_rows{i}", [P, D], F32) for i in range(NT)]
        for t in y_rows:
            y_cleared = pool.mark(POOL.memset(t[:], 0.0))

        def gate_up_product(n, wu, xs, width, w_ready, x_ready):
            hi, lo = (t[:, :, 0:width] for t in hT[n % 2])
            for j in range(KF):
                banks = []
                for which in range(2):
                    bk = next_bank()
                    banks.append(bk)
                    wait(PE, w_ready[which], x_ready, bank_free[bk])
                    w = [t[:].rearrange("p (k f) -> p k f", k=KD) for t in wu[which]]
                    for k in range(KD):
                        for i, (a, x) in enumerate(((0, 0), (0, 1), (1, 0))):
                            mm = PE.matmul(bank[bk][:, 0:width], w[a][:, k, P * j:P * j + P], xs[x][:, k, :],
                                           start=(k == 0 and i == 0), stop=(k == KD - 1 and i == 2))
                    m = pe.mark(mm)
                    between()
                    h = hidden[j % 2][:, 0:width]
                    if which == 0:
                        wait(ACTE, m, hidden_free[j % 2])
                        m = bank_free[bk] = act.mark(ACTE.activation(h, bank[bk][:, 0:width], ACT.Silu))
                        wait(DVE, m)
                    else:
                        wait(DVE, m)
                        m = bank_free[bk] = dve.mark(DVE.tensor_tensor(h, bank[bk][:, 0:width], h, MULT))
                wait(ACTE, m, hT_free[n % 2])
                high = act.mark(ACTE.activation(hi[:, j, :], h, ACT.Copy))
                wait(DVE, high)
                hidden_free[j % 2] = low = dve.mark(DVE.tensor_tensor(
                    lo[:, j, :], h, hi[:, j, :].bitcast(F32), SUB))
            return low

        hidden_free = [None] * 2
        hT_free = [None] * 2

        def down_product(n, wd, r0, n_r, bk, w_ready, h_ready, first, last):
            hi, lo = hT[n % 2]
            wait(PE, w_ready, h_ready, bank_free[bk])
            w = [t[:].rearrange("p (k n) -> p k n", k=KF) for t in wd]
            for j in range(KF):
                for i, (h, a) in enumerate(((hi, 0), (hi, 1), (lo, 0))):
                    mm = PE.matmul(bank[bk][0:n_r, :], h[:, j, r0:r0 + n_r], w[a][:, j, :],
                                   start=(first and j == 0 and i == 0),
                                   stop=(last and j == KF - 1 and i == 2))
            return pe.mark(mm)

        stream.load(NRAW)
        routes = (step for c in range(1, NCH) for step in route(c))

        pace = [0, 2, 3, 3]

        def beside_shared():
            for _ in range(pace.pop(0) if pace else 2):
                next(routes, None)

        between = beside_shared
        x2_done = [None] * B
        x2_out = counter("x2_out")

        def shared_down(n, q, c, h_ready):
            for j in range(CT):
                b = CT * c + j
                bk = 4 + (CT * n + j) % 4
                m = down_product(n, w_split[q % NUNIT][2], N * j, N, bk, stream.ready[3 * q + 2],
                                 h_ready, True, True)
                between()
                wait(DVE, m, xs_done[c], x2_done[b])
                x2_done[b] = bank_free[bk] = dve.mark(DVE.scalar_tensor_tensor(
                    out=x_all[:, b, :], in0=bank[bk][0:N, :], scalar=gates[0:N, 1:2],
                    in1=x_all[:, b, :], op0=MULT, op1=ADD))
            hT_free[n % 2] = m
            if c == NCH - 1:
                stream.unit_free[q % NUNIT] = m
            if q == NQ - 1:
                wait(ACTE, x2_done[CT * c + CT - 1])
                small_free["x2"] = x2_out.mark(ACTE.dma_start(
                    x2_rows[CW * c:CW * c + CW, :].rearrange("(b n) d -> n b d", n=N),
                    x_all[:, CT * c:CT * c + CT, :]), 16)

        class Sweep:

            def __init__(self, index, stream, first_unit, sems, rows_free, xsT_free, ids_wait, x2_wait):
                self.stream, self.u0, self.x2_wait = stream, first_unit, x2_wait
                ids_io, *self.y_io = sems[:1 + 2 * NT]
                self.rows_in = sems[1 + 2 * NT:]
                self.rows_free, self.xsT_free, self.y_free = rows_free, xsT_free, [None] * NT
                self.gathered, self.x_ready, self.residual = {}, {}, [None] * NT
                by_sweep = lists.rearrange("(e s p i) o -> p e s (i o)", e=E, s=MAX_SWEEPS, i=NT)
                wait(ACTE, ids_wait)
                self.ids_ready = ids_io.mark(ACTE.dma_start(
                    list_ids[:], by_sweep[:, :, index, :].rearrange("p e s i -> p (e s) i")), 16)

            def gather(self, e):
                wait(POOL, self.ids_ready)
                for i in range(NT):
                    r = (NT * e + i) % 4
                    wait(POOL, self.rows_free[r])
                    self.gathered[e, i] = self.rows_in[r].mark(POOL.indirect_dma_start(
                        rows[r][:], None, gated_rows,
                        bass.IndirectOffsetOnAxis(ap=list_ids[:, e, i:i + 1], axis=0),
                        bounds_check=T - 1, oob_is_err=False), 16)

            def transpose_expert(self, e):
                for i in range(NT):
                    r = (NT * e + i) % 4
                    self.x_ready[e], self.rows_free[r] = transpose_rows(
                        rows[r][:], P, [t[:, :, P * i:P * i + P] for t in xnT[e % 2]],
                        self.gathered[e, i], self.xsT_free[e % 2])

            def gather_residual(self, e):
                wait(POOL, self.x2_wait, y_cleared)
                for i in range(NT):
                    wait(POOL, self.y_free[i])
                    self.residual[i] = self.y_io[i].mark(POOL.indirect_dma_start(
                        y_rows[i][:], None, x2_rows,
                        bass.IndirectOffsetOnAxis(ap=list_ids[:, e, i:i + 1], axis=0),
                        bounds_check=T - 1, oob_is_err=False), 16)

            def down(self, n, e, q, h_ready):
                u = self.u0 + n
                for i in range(NT):
                    bk = 4 + NT * (e % 2) + i
                    m = down_product(n, w_split[u % NUNIT][2], P * i, P, bk, self.stream.ready[3 * u + 2],
                                     h_ready, q == 0, q == NQ - 1)
                    between()
                    if q == NQ - 1:
                        wait(DVE, m, self.residual[i])
                        bank_free[bk] = added = dve.mark(DVE.scalar_tensor_tensor(
                            out=y_rows[i][:], in0=bank[bk][:], scalar=gates[:, 1:2],
                            in1=y_rows[i][:], op0=MULT, op1=ADD))
                        wait(POOL, added)
                        self.y_free[i] = self.y_io[NT + i].mark(POOL.indirect_dma_start(
                            out_rows, bass.IndirectOffsetOnAxis(ap=list_ids[:, e, i:i + 1], axis=0),
                            y_rows[i][:], None, bounds_check=T - 1, oob_is_err=False), 16)
                hT_free[n % 2] = self.stream.unit_free[u % NUNIT] = m

            def run(self, down_before):
                for n, (e, q) in enumerate((e, q) for e in range(E) for q in range(NQ)):
                    if q == 0 and e + 1 < E:
                        self.gather(e + 1)
                    if q == 1:
                        self.gather_residual(e)
                    if q == NQ - 1 and e + 1 < E:
                        self.transpose_expert(e + 1)
                    u = self.u0 + n
                    h_ready = gate_up_product(
                        n, w_split[u % NUNIT], [t[:, :, 0:SLOTS] for t in xnT[e % 2]], SLOTS,
                        [self.stream.ready[3 * u], self.stream.ready[3 * u + 1]], self.x_ready[e])
                    if q == NQ - 1:
                        self.xsT_free[e % 2] = (pe, pe.value)
                    if down_before:
                        down_before()
                    down_before = lambda n=n, e=e, q=q, h=h_ready: self.down(n, e, q, h)
                down_before()

        def splits(stream):
            while True:
                stream.split(1)
                yield
                yield

        def sweep_semaphores(name):
            return ([counter(f"{name}_{n}") for n in ["ids"] + [f"residual{i}" for i in range(NT)]
                     + [f"y_out{i}" for i in range(NT)]] + [counter(f"{name}_rows{i}") for i in range(4)])

        def count_sweeps():
            bk = next_bank()
            wait(PE, small_free["counts"], bank_free[bk])
            m = pe.mark(PE.matmul(bank[bk][0:N, 0:E], ones16[:], counted[:, NCH % 2, :], start=True, stop=True))
            wait(DVE, m)
            bank_free[bk] = m = dve.mark(DVE.tensor_reduce(sweeps_f[:, 0:1], bank[bk][0:1, 0:E], AX.X, ALU.max))
            wait(DVE, m)
            m = dve.mark(DVE.tensor_scalar(sweep_edges[:], sweep_edges[:], sweeps_f[:, 0:1], None, ALU.is_lt))
            wait(DVE, m)
            m = dve.mark(DVE.tensor_reduce(sweeps_f[:, 1:2], sweep_edges[:], AX.X, ADD))
            wait(DVE, m)
            sweeps_ready = dve.mark(DVE.tensor_copy(sweeps[:], sweeps_f[:, 1:2]))
            return sweeps_ready

        down_before = None
        xnT_free = {}
        for n, (q, c) in enumerate((q, c) for q in range(NQ) for c in range(NCH)):
            h_ready = gate_up_product(n, w_split[q % NUNIT], [t[:] for t in xnT[c]], CW,
                                      [stream.ready[3 * q], stream.ready[3 * q + 1]], xnT_ready[c])
            xnT_free[c] = (pe, pe.value)
            if down_before:
                down_before()
            down_before = lambda n=n, q=q, c=c, h=h_ready: shared_down(n, q, c, h)
            if c > 0 or q == 0:
                stream.split(1)
            if (q, c) == (NQ - 1, 1):
                first = Sweep(slice(0, 1), stream, NQ, sweep_semaphores("first"), rows_free,
                              [xnT_free[0], xnT_free[1]], small_free["table"], None)
                first.gather(0)
            if (q, c) == (NQ - 1, 2):
                first.transpose_expert(0)
            if (q, c) == (1, NCH - 1):
                sweeps_ready = count_sweeps()

        between = splits(stream).__next__

        def last_shared():
            shared_last()
            first.x2_wait = small_free["x2"]

        shared_last = down_before
        first.run(last_shared)

        for e in (PE, ACTE, DVE, POOL, SP):
            wait(e, sweeps_ready)
        wait(POOL, *first.y_free)
        wait(SP, *first.y_free)
        further = nc.values_load(sweeps[0:1, 0:1], min_val=0, max_val=MAX_SWEEPS - 1)
        loop_sems = [counter(f"loop_{n}") for n in ("pe", "act", "dve")]
        loop_sweep = sweep_semaphores("loop")
        loop_raw = [counter(f"loop_raw{i}") for i in range(NRAW)]
        with nc.If(further):
            nc.all_engine_barrier()
            with nc.Fori(0, further) as sweep:
                wait = Waits()
                pe, act, dve = loop_sems
                y_cleared = None
                bank_free = [None] * 8
                hidden_free, hT_free = [None] * 2, [None] * 2
                loop_stream = WeightStream(expert_parts, loop_raw, wait, act, dve)
                again = Sweep(bass.ds(sweep + 1, 1), loop_stream, 0, loop_sweep, [None] * 4,
                              [None] * 2, None, None)
                again.gather(0)
                loop_stream.split(3)
                again.transpose_expert(0)
                between = splits(loop_stream).__next__
                again.run(None)
                wait(POOL, *again.y_free, *again.gathered.values())
                wait(SP, *again.y_free)
                nc.all_engine_barrier()
                POOL.dma_reset()
                for c in loop_sems + loop_sweep + loop_raw:
                    POOL.sem_clear(c.sem)
                nc.all_engine_barrier()


_INS = ["x", "ctx_2048", "g_xattn", "g_ffn", "L0_xattn_Wq", "L0_xattn_Wk", "L0_xattn_Wv",
        "L0_ffn_router_w", "L0_ffn_w_gate_up", "L0_ffn_w_down", "L0_ffn_shared_gate_up",
        "L0_ffn_shared_down"]


def kernel(**inputs):
    import numpy as np
    import concourse.bacc as bacc
    from concourse.bass_utils import run_bass_kernel_spmd

    nc = bacc.Bacc("TRN2", target_bir_lowering=False, num_devices=1)
    arrays, args = {}, []
    for name in _INS:
        arrays[name] = np.ascontiguousarray(inputs[name])
        args.append(nc.dram_tensor(name, arrays[name].shape, mybir.dt.from_np(arrays[name].dtype),
                                   kind="ExternalInput").ap())
    out = nc.dram_tensor("out", arrays["x"].shape, F32, kind="ExternalOutput").ap()
    build_program(nc, *args, out)
    result = run_bass_kernel_spmd(nc, [arrays], core_ids=[0])
    return result.results[0]["out"]
```
